# Optimizing a Trainium2 kernel written in Bass

```python
import numpy as np
import jax
import jax.numpy as jnp

def _softmax(x, axis=-1):
    return jax.nn.softmax(x, axis=axis)

def _gelu(x):
    return jax.nn.gelu(x, approximate=True)

def _silu(x):
    return jax.nn.silu(x)

def _sigmoid(x):
    return jax.nn.sigmoid(x)

def _layernorm(x, axis=-1, eps=1e-05):
    m = jnp.mean(x, axis=axis, keepdims=True)
    v = jnp.var(x, axis=axis, keepdims=True)
    return (x - m) / jnp.sqrt(v + eps)

def _scatter_add(tgt, idx, src, axis=0):
    return tgt.at[idx].add(src)

def _segment_sum(src, seg, n):
    return jax.ops.segment_sum(src, seg, n)
kernel_name = 'mk_vit_tower_d1_tok_img768_r4_e5d518'

def setup_inputs(seed: int=0):
    np.random.seed(seed)
    _w = jnp.asarray

    def _rec_inputs():
        import jax
        import jax.numpy as jnp
        _rk = jax.random.key(seed)
        x = -0.000125008 + 0.999885 * jax.random.normal(jax.random.fold_in(_rk, 1), (16, 2, 128, 128), jnp.float32)
        return x
    x = _rec_inputs()

    def _L0_tok_setup():
        import jax, jax.numpy as jnp
        import numpy as np
        PATCH = 16

        def _patchify(x, p):
            B, C, H, W = x.shape
            nh, nw = (H // p, W // p)
            patch_dim = C * p * p
            x = x.reshape(B, C, nh, p, nw, p)
            x = jnp.transpose(x, (0, 1, 2, 4, 3, 5))
            return x.reshape(B, -1, patch_dim)
        key = jax.random.key(seed)
        k1, k2, k3, k4 = jax.random.split(key, 4)
        B, C, H, W = (64, 2, 128, 128)
        dim = 192
        num_patches = H // PATCH * (W // PATCH)
        patch_dim = C * PATCH * PATCH
        x = jax.random.normal(k1, (B, C, H, W), dtype=jnp.float32)
        proj_w = jax.random.normal(k2, (dim, patch_dim), dtype=jnp.float32) * 0.02
        proj_b = jax.random.normal(k3, (dim,), dtype=jnp.float32) * 0.02
        pos_emb = jax.random.normal(k4, (1, num_patches, dim), dtype=jnp.float32) * 0.02
        return {'x': x, 'proj_w': proj_w, 'proj_b': proj_b, 'pos_emb': pos_emb}
    _L0_tok_all = _L0_tok_setup()
    _L0_tok_in = {k: v for k, v in _L0_tok_all.items() if k in ('proj_w', 'proj_b', 'pos_emb')}
    del _L0_tok_all

    def _L0_attn_setup():
        import jax, jax.numpy as jnp
        import numpy as np

        def silu(x):
            return x * jax.nn.sigmoid(x)
        key = jax.random.key(seed)
        ks = jax.random.split(key, 12)
        B, S, Dm = (2, 512, 192)
        I, N, R, K = (384, 16, 48, 4)
        s = 0.02
        return {'input_states': jax.random.normal(ks[0], (B, S, Dm), jnp.float32), 'in_proj_w': jax.random.normal(ks[1], (2 * I, Dm), jnp.float32) * s, 'conv_w': jax.random.normal(ks[2], (I, 1, K), jnp.float32) * s, 'conv_b': jax.random.normal(ks[3], (I,), jnp.float32) * s, 'x_proj_w': jax.random.normal(ks[4], (R + 2 * N, I), jnp.float32) * s, 'dt_proj_w': jax.random.normal(ks[5], (I, R), jnp.float32) * s, 'dt_proj_b': jax.random.normal(ks[6], (I,), jnp.float32) * s, 'A_log': jax.random.normal(ks[7], (I, N), jnp.float32) * 0.5, 'D': jax.random.normal(ks[8], (I,), jnp.float32) * s, 'out_proj_w': jax.random.normal(ks[9], (Dm, I), jnp.float32) * s, 'alpha': jax.random.uniform(ks[10], (I,), jnp.float32), 'feature_gating': jax.random.uniform(ks[11], (I,), jnp.float32)}
    _L0_attn_all = _L0_attn_setup()
    _L0_attn_in = {k: v for k, v in _L0_attn_all.items() if k in ('in_proj_w', 'conv_w', 'conv_b', 'x_proj_w', 'dt_proj_w', 'dt_proj_b', 'A_log', 'D', 'out_proj_w', 'alpha', 'feature_gating')}
    del _L0_attn_all

    def _L0_ffn_setup():
        import jax, jax.numpy as jnp
        import numpy as np
        DIM = 192
        HID = 512
        E = 8
        TOP_K = 2

        def _ffn(t, a, b, c):
            return jax.nn.silu(t @ a.T) * (t @ c.T) @ b.T
        key = jax.random.key(seed)
        ks = jax.random.split(key, 9)
        s = 0.02
        return {'x': jax.random.normal(ks[0], (2, 256, DIM), dtype=jnp.float32), 'gate_w': jax.random.normal(ks[1], (E, DIM), dtype=jnp.float32) * s, 'w1': jax.random.normal(ks[2], (E, HID, DIM), dtype=jnp.float32) * s, 'w2': jax.random.normal(ks[3], (E, DIM, HID), dtype=jnp.float32) * s, 'w3': jax.random.normal(ks[4], (E, HID, DIM), dtype=jnp.float32) * s, 'ws1': jax.random.normal(ks[5], (HID, DIM), dtype=jnp.float32) * s, 'ws2': jax.random.normal(ks[6], (DIM, HID), dtype=jnp.float32) * s, 'ws3': jax.random.normal(ks[7], (HID, DIM), dtype=jnp.float32) * s}
    _L0_ffn_all = _L0_ffn_setup()
    _L0_ffn_in = {k: v for k, v in _L0_ffn_all.items() if k in ('gate_w', 'w1', 'w2', 'w3', 'ws1', 'ws2', 'ws3')}
    del _L0_ffn_all
    return {'x': x, 'L0_tok_proj_w': _L0_tok_in['proj_w'], 'L0_tok_proj_b': _L0_tok_in['proj_b'], 'L0_tok_pos_emb': _L0_tok_in['pos_emb'], 'L0_attn_in_proj_w': _L0_attn_in['in_proj_w'], 'L0_attn_conv_w': _L0_attn_in['conv_w'], 'L0_attn_conv_b': _L0_attn_in['conv_b'], 'L0_attn_x_proj_w': _L0_attn_in['x_proj_w'], 'L0_attn_dt_proj_w': _L0_attn_in['dt_proj_w'], 'L0_attn_dt_proj_b': _L0_attn_in['dt_proj_b'], 'L0_attn_A_log': _L0_attn_in['A_log'], 'L0_attn_D': _L0_attn_in['D'], 'L0_attn_out_proj_w': _L0_attn_in['out_proj_w'], 'L0_attn_alpha': _L0_attn_in['alpha'], 'L0_attn_feature_gating': _L0_attn_in['feature_gating'], 'L0_ffn_gate_w': _L0_ffn_in['gate_w'], 'L0_ffn_w1': _L0_ffn_in['w1'], 'L0_ffn_w2': _L0_ffn_in['w2'], 'L0_ffn_w3': _L0_ffn_in['w3'], 'L0_ffn_ws1': _L0_ffn_in['ws1'], 'L0_ffn_ws2': _L0_ffn_in['ws2'], 'L0_ffn_ws3': _L0_ffn_in['ws3']}

def reference(x, L0_tok_proj_w, L0_tok_proj_b, L0_tok_pos_emb, L0_attn_in_proj_w, L0_attn_conv_w, L0_attn_conv_b, L0_attn_x_proj_w, L0_attn_dt_proj_w, L0_attn_dt_proj_b, L0_attn_A_log, L0_attn_D, L0_attn_out_proj_w, L0_attn_alpha, L0_attn_feature_gating, L0_ffn_gate_w, L0_ffn_w1, L0_ffn_w2, L0_ffn_w3, L0_ffn_ws1, L0_ffn_ws2, L0_ffn_ws3):
    import jax
    import jax.numpy as jnp

    def _L0_tok_ref(x, proj_w, proj_b, pos_emb):
        import jax, jax.numpy as jnp
        import numpy as np
        PATCH = 16

        def _patchify(x, p):
            B, C, H, W = x.shape
            nh, nw = (H // p, W // p)
            patch_dim = C * p * p
            x = x.reshape(B, C, nh, p, nw, p)
            x = jnp.transpose(x, (0, 1, 2, 4, 3, 5))
            return x.reshape(B, -1, patch_dim)
        patches = _patchify(x, PATCH)
        out = jnp.einsum('bnp,dp->bnd', patches, proj_w) + proj_b
        return out + pos_emb

    def _L0_attn_ref(input_states, in_proj_w, conv_w, conv_b, x_proj_w, dt_proj_w, dt_proj_b, A_log, D, out_proj_w, alpha, feature_gating):
        import jax, jax.numpy as jnp
        import numpy as np

        def silu(x):
            return x * jax.nn.sigmoid(x)
        Bsz, S, _ = input_states.shape
        I, N = A_log.shape
        R = dt_proj_w.shape[1]
        K = conv_w.shape[-1]
        proj = jnp.einsum('bsd,ed->bse', input_states, in_proj_w)
        hidden, gate = jnp.split(proj.transpose(0, 2, 1), 2, axis=1)
        h = jax.lax.conv_general_dilated(hidden, conv_w, window_strides=(1,), padding=[(K - 1, 0)], dimension_numbers=('NCH', 'OIH', 'NCH'), feature_group_count=I)
        h = silu(h + conv_b[None, :, None])
        ssm_p = jnp.einsum('bis,ei->bse', h, x_proj_w)
        ts, Bm, Cm = jnp.split(ssm_p, [R, R + N], axis=-1)
        dt = jax.nn.softplus(jnp.einsum('bsr,ir->bsi', ts, dt_proj_w) + dt_proj_b)
        dt = dt.transpose(0, 2, 1)
        dt = dt.at[:, :, -1].multiply(alpha[None, :])
        A = -jnp.exp(A_log.astype(jnp.float32))
        dA = jnp.exp(A[None, :, None, :] * dt[:, :, :, None])
        dBu = dt[:, :, :, None] * Bm[:, None, :, :] * h[:, :, :, None]

        def step(state, xs):
            dA_t, dBu_t, C_t = xs
            state = dA_t * state + dBu_t
            y = jnp.einsum('bin,bn->bi', state, C_t)
            return (state, y)
        init = jnp.zeros((Bsz, I, N), input_states.dtype)
        _, ys = jax.lax.scan(step, init, (dA.transpose(2, 0, 1, 3), dBu.transpose(2, 0, 1, 3), Cm.transpose(1, 0, 2)))
        y = ys.transpose(1, 2, 0)
        y = (y + h * D[None, :, None]) * silu(gate)
        y = y.at[:, :, -1].multiply(feature_gating[None, :])
        return jnp.einsum('bis,di->bsd', y, out_proj_w)

    def _L0_ffn_ref(x, gate_w, w1, w2, w3, ws1, ws2, ws3):
        import jax, jax.numpy as jnp
        import numpy as np
        DIM = 192
        HID = 512
        E = 8
        TOP_K = 2

        def _ffn(t, a, b, c):
            return jax.nn.silu(t @ a.T) * (t @ c.T) @ b.T
        B, S, D = x.shape
        xf = x.reshape(-1, D)
        T = xf.shape[0]
        logits = xf @ gate_w.T
        scores = jax.nn.softmax(logits, axis=-1)
        topk_w, topk_idx = jax.lax.top_k(scores, TOP_K)
        topk_w = topk_w / (topk_w.sum(-1, keepdims=True) + 1e-20)
        cw = jnp.zeros((T, E), xf.dtype).at[jnp.arange(T)[:, None], topk_idx].add(topk_w)
        y = jnp.zeros_like(xf)
        for e in range(E):
            y = y + cw[:, e:e + 1] * _ffn(xf, w1[e], w2[e], w3[e])
        y = y + _ffn(xf, ws1, ws2, ws3)
        return y.reshape(B, S, D)
    h = _L0_tok_ref(x, L0_tok_proj_w, L0_tok_proj_b, L0_tok_pos_emb)
    h = h + _L0_attn_ref(_layernorm(h, axis=-1), L0_attn_in_proj_w, L0_attn_conv_w, L0_attn_conv_b, L0_attn_x_proj_w, L0_attn_dt_proj_w, L0_attn_dt_proj_b, L0_attn_A_log, L0_attn_D, L0_attn_out_proj_w, L0_attn_alpha, L0_attn_feature_gating)
    h = h + _L0_ffn_ref(_layernorm(h, axis=-1), L0_ffn_gate_w, L0_ffn_w1, L0_ffn_w2, L0_ffn_w3, L0_ffn_ws1, L0_ffn_ws2, L0_ffn_ws3)
    return h

_drawn_inputs = setup_inputs


def setup_inputs(seed=0):
    import zlib

    import numpy as np

    out = dict(_drawn_inputs(seed))
    spreads = {}
    factors = {'L0_attn_in_proj_w': 8.0,
     'L0_attn_conv_w': 8.0,
     'L0_attn_conv_b': 8.0,
     'L0_attn_x_proj_w': 8.0,
     'L0_attn_dt_proj_w': 8.0,
     'L0_attn_dt_proj_b': 8.0,
     'L0_attn_A_log': 8.0,
     'L0_attn_D': 64.0,
     'L0_attn_out_proj_w': 8.0,
     'L0_attn_alpha': 8.0,
     'L0_attn_feature_gating': 8.0,
     'L0_ffn_gate_w': 8.0,
     'L0_ffn_w1': 8.0,
     'L0_ffn_w2': 8.0,
     'L0_ffn_w3': 8.0,
     'L0_ffn_ws1': 8.0,
     'L0_ffn_ws2': 8.0,
     'L0_ffn_ws3': 8.0}
    for name, (base, spread) in spreads.items():
        noise = np.random.default_rng([zlib.crc32(name.encode()), seed]).standard_normal(out[name].shape)
        drawn = base * np.exp(spread * noise) if base else spread * noise
        out[name] = jnp.asarray(drawn.astype(out[name].dtype))
    for name, factor in factors.items():
        out[name] = (out[name] * factor).astype(out[name].dtype)
    return out
```

```python
import numpy as np
import concourse.bass as bass
import concourse.mybir as mybir
from concourse.alu_op_type import AluOpType as ALU
from contextlib import ExitStack

F32 = mybir.dt.float32
I32 = mybir.dt.int32
U32 = mybir.dt.uint32
ACT = mybir.ActivationFunctionType
AX = mybir.AxisListType

B, C_IN, IMG, PATCH = 16, 2, 128, 16
S = (IMG // PATCH) ** 2
D = 192
DA, DB = 128, D - 128
PD = C_IN * PATCH * PATCH
PK = PD // 128
T = B * S
TT = T // 128
G = 2
GT = T // G
GB = B // G
TPG = TT // G
I = 384
IC = I // 128
N = 16
R = 48
K = 4
NQ = 4
Q = N // NQ
E = 8
HID = 512
HC = HID // 128
SLOT_TILES = 2 * T // 128 + E
TILES = TT + SLOT_TILES
EPS = 1e-5
PARAMS = K + 1 + 1 + N + 1 + 1 + 1
P_CW, P_CB, P_DTB, P_A, P_D, P_ALPHA, P_FG = 0, K, K + 1, K + 2, K + 2 + N, K + 3 + N, K + 4 + N


def program(nc, xT_d, projT_d, projb_d, pos_d, inT_d, par_d, xpT_d, dtT_d, outT_d, gateT_d, w13T_d, w2T_d, out_d):
    ctx = ExitStack()
    with ctx:
        def sb(name, shape, dt=F32):
            return ctx.enter_context(nc.sbuf_tensor(name, shape, dt))

        def sem(name):
            return ctx.enter_context(nc.semaphore(name))

        bc_d = nc.dram_tensor("bc_scratch", [2, G * N, GT], F32).ap()
        rows_d = nc.dram_tensor("rows_scratch", [TILES * 128, D], F32).ap()
        y_d = nc.dram_tensor("y_scratch", [TILES * 128, D], F32).ap()

        projT = sb("projT", [128, PK, D])
        inTa = sb("inTa", [DA, 2 * I])
        inTb = sb("inTb", [DB, 2 * I])
        par = sb("par", [128, IC, PARAMS])
        negA = sb("negA", [128, IC, N])
        diagD = sb("diagD", [128, IC, 128])
        xpT = sb("xpT", [128, IC, R + 2 * N])
        dtT = sb("dtT", [R, I])
        outT = sb("outT", [128, IC, D])
        gateTa = sb("gateTa", [DA, E])
        gateTb = sb("gateTb", [DB, E])
        EW = 4 * HID + HC * D
        experts = sb("experts", [128, E + 1, EW])
        w13a = experts[0:DA, :, 0:2 * HID]
        w13b = experts[0:DB, :, 2 * HID:4 * HID]
        w2 = experts[:, :, 4 * HID:EW]
        LATE = range(2, E)
        late = experts[:, 2:E, :].rearrange("p e n -> p (e n)")
        ident = sb("ident", [128, 128])
        ones = sb("ones", [128, 128])
        before = sb("before", [128, 128])
        iota_i = sb("iota_i", [128, SLOT_TILES], I32)
        iota = sb("iota", [128, SLOT_TILES])
        steps = sb("steps", [128, TT])
        neghalf = sb("neghalf", [128, TPG])
        posb = sb("posb", [128, D])
        projb = sb("projb", [128, D])
        h0 = sb("h0", [128, TT, D])
        xn = sb("xn", [128, TT, D])
        stats = sb("stats", [128, TT, 6])
        mv = sb("mv", [128, TT, 2])
        veps = sb("veps", [128, TT])
        rstd = sb("rstd", [128, TT])
        xnTa = sb("xnTa", [DA, T])
        xnTb = sb("xnTb", [DB, T])
        ssm = sb("ssm", [R + 2 * N, G, GT])
        h = sb("h", [128, G, IC, GT])
        dt = sb("dt", [128, G, IC, GT])
        u = sb("u", [128, G, IC, GT])
        sg = sb("sg", [128, G, IC, GT])
        lg = sb("lg", [128, TT, E])
        sc = sb("sc", [128, TT, E])
        red = sb("red", [128, 4, TT])
        m8 = sb("m8", [128, TT, 8])
        ix = sb("ix", [128, TT, 8], U32)
        ixf = sb("ixf", [128, 2, TT])
        wk = sb("wk", [128, 2, TT])
        hot = sb("hot", [128, 2, TT, E])
        msum = sb("msum", [128, TT, E])
        mcum = sb("mcum", [128, TT + 1, E])
        rank = sb("rank", [128, TT, E])
        cnt = sb("cnt", [128, E])
        gt = sb("gt", [128, E * TT])
        ntile = sb("ntile", [128, E])
        tend = sb("tend", [128, E])
        base = sb("base", [128, E])
        posf = sb("posf", [128, 2, TT])
        pos_i = sb("pos_i", [128, 2, TT], I32)
        tcmp = sb("tcmp", [128, SLOT_TILES, E])
        tef = sb("tef", [128, TILES])
        te = sb("te", [128, TILES], I32)
        xs = sb("xs", [128, 2, D])
        xsTa = sb("xsTa", [DA, 2, 128])
        xsTb = sb("xsTb", [DB, 2, 128])
        RING = 4 * NQ * GT
        assert 2 * RING <= len(LATE) * EW
        ring = late[:, 0:RING].rearrange("p (r n) -> p r n", r=4)
        state2 = sb("state2", [128, NQ * GT])
        zeros = state2[:, 0:4 * D]
        bc = late[:, RING:2 * RING].rearrange("p (r b q t) -> p r b q t", r=2, b=2, q=NQ)
        xT = bc[:, :, :, :, :].rearrange("p a b q t -> p (a b q t)")[:, 0:PK * T].rearrange("p (k t) -> p k t", k=PK)
        hp = ring[:, :, :].rearrange("p r n -> p (r n)")[:, 0:G * IC * GB * (S + K - 1)].rearrange(
            "p (g i b s) -> p g i b s", g=G, i=IC, b=GB)
        hflat = h[:, :, :, :].rearrange("p g i t -> p (g i t)")
        sa = hflat[:, 0:2 * HID].rearrange("p (r n) -> p r n", r=2)
        hm = hflat[:, 2 * HID:4 * HID].rearrange("p (r n) -> p r n", r=2)
        hT = hflat[:, 4 * HID:6 * HID].rearrange("p (r c n) -> p r c n", r=2, c=HC)
        uflat = u[:, :, :, :].rearrange("p g i t -> p (g i t)")
        ysb = uflat[:, 0:2 * D].rearrange("p (r n) -> p r n", r=2)
        yg = [dt[:, :, :, :].rearrange("p g i t -> p (g i t)")[:, 0:TT * D].rearrange("p (t d) -> p t d", t=TT),
              uflat[:, 2 * D:(TT + 2) * D].rearrange("p (t d) -> p t d", t=TT),
              sg[:, :, :, :].rearrange("p g i t -> p (g i t)")[:, 0:TT * D].rearrange("p (t d) -> p t d", t=TT)]

        ps = ctx.enter_context(nc.psum_tensor("ps", [128, 8, 512], F32))

        def decay(r):
            return ring[:, r, :].rearrange("p (n b s) -> p n b s", n=NQ, b=GB)

        def state(r):
            return ring[:, 2 + r, :] if r < 2 else state2[:, :]

        ld_x = [sem(f"ld_x{g}") for g in range(G)]
        ld_proj = sem("ld_proj")
        ld_par = sem("ld_par")
        ld_mid = sem("ld_mid")
        ld_w = sem("ld_w")
        ident_ok = sem("ident_ok")
        pool_c = sem("pool_c")
        dve_c = sem("dve_c")
        act_c = sem("act_c")
        consts_ok = sem("consts_ok")
        patch_mm = sem("patch_mm")
        h0_ok = sem("h0_ok")
        aggr_ok = sem("aggr_ok")
        rstd_ok = sem("rstd_ok")
        xn_ok = sem("xn_ok")
        xn_tr = sem("xn_tr")
        xnT_ok = sem("xnT_ok")
        in_mm = sem("in_mm")
        in_used = sem("in_used")
        pads_ok = sem("pads_ok")
        hidden_ok = sem("hidden_ok")
        conv_ok = sem("conv_ok")
        h_ok = sem("h_ok")
        xp_mm = sem("xp_mm")
        ssm_ok = sem("ssm_ok")
        bc_st = [sem(f"bc_st{g}") for g in range(G)]
        bc_ld = [sem(f"bc_ld{r}") for r in range(2)]
        dt_mm = sem("dt_mm")
        dt_lin = sem("dt_lin")
        lnp_ok = sem("lnp_ok")
        expA_ok = sem("expA_ok")
        negA_ok = sem("negA_ok")
        diag_ok = sem("diag_ok")
        dt_ok = sem("dt_ok")
        u_ok = sem("u_ok")
        decay_free = sem("decay_free")
        state_free = sem("state_free")
        decay_ok = sem("decay_ok")
        dbu_ok = sem("dbu_ok")
        cs_ok = sem("cs_ok")
        yevac = sem("yevac")
        y_ok = sem("y_ok")
        op_mm = sem("op_mm")
        h1_ok = sem("h1_ok")
        zero_ok = sem("zero_ok")
        zero_st = sem("zero_st")
        lg_mm = sem("lg_mm")
        lmax_ok = sem("lmax_ok")
        lexp_ok = sem("lexp_ok")
        mcum_ok = sem("mcum_ok")
        rank_mm = sem("rank_mm")
        pos_ok = sem("pos_ok")
        te_ok = sem("te_ok")
        scat_st = sem("scat_st")
        xs_ld = [sem(f"xs_ld{r}") for r in range(2)]
        xs_tr = sem("xs_tr")
        xsT_ok = sem("xsT_ok")
        up_a = sem("up_a")
        up_c = sem("up_c")
        sa_ok = sem("sa_ok")
        hm_ok = sem("hm_ok")
        hm_tr = sem("hm_tr")
        hT_ok = sem("hT_ok")
        down_mm = sem("down_mm")
        ysb_ok = sem("ysb_ok")
        y_st = [sem(f"y_st{r}") for r in range(2)]
        sh_ld = sem("sh_ld")
        gat_ld = sem("gat_ld")
        fin_ok = sem("fin_ok")
        out_st = sem("out_st")

        STEPS = Q * IC
        YBANK = (4, 1)
        OBANK = (0, 7)
        rows_v = rows_d.rearrange("(s p) d -> s p d", p=128)
        y_v = y_d.rearrange("(s p) d -> s p d", p=128)
        out_v = out_d.rearrange("(s p) d -> s p d", p=128)

        def wait(eng, signal, count):
            if not isinstance(count, int) or count > 0:
                eng.wait_ge(signal, count)

        block = ctx.enter_context(nc.Block())

        def stage_loop(eng, parts, routed_ready=None):
            def step(s, r, ends):
                for lag, part in parts:
                    if not ends or 0 <= s + lag < TILES:
                        part(s + lag, (r + lag) % 2)

            for s in range(-2, TT):
                if s == TT - 2 and routed_ready:
                    routed_ready()
                step(s, s % 2, True)
            with eng.Fori(0, (TILES - TT - 2) // 2) as j:
                for r in range(2):
                    step(j * 2 + (r + TT), r, False)
            for s in range(TILES - 2, TILES + 1):
                step(s, s % 2, True)

        @block.sync
        def _(sp):
            xT_v = xT_d.rearrange("(k p) t -> p k t", p=128)
            sp.dma_start(xT[:, :, 0:GT], xT_v[:, :, 0:GT]).then_inc(ld_x[0], 16)
            sp.dma_start(xT[:, :, GT:T], xT_v[:, :, GT:T]).then_inc(ld_x[1], 16)
            def load_expert(e):
                sp.dma_start(w13a[:, e, :], w13T_d[e, 0:DA, :]).then_inc(ld_w, 16)
                sp.dma_start(w13b[:, e, :], w13T_d[e, DA:D, :]).then_inc(ld_w, 16)
                sp.dma_start(w2[:, e, :].rearrange("p (c d) -> p c d", c=HC),
                             w2T_d[e].rearrange("(c p) d -> p c d", p=128)).then_inc(ld_w, 16)

            def load_quad(z, r):
                for b in range(2):
                    sp.dma_start(bc[:, r, b, :, :],
                                 bc_d[b].rearrange("(z q) t -> z q t", q=NQ)[z].partition_broadcast(128)
                                 ).then_inc(bc_ld[r], 16)

            for g in range(G):
                sp.wait_ge(ssm_ok, g + 1)
                for b in range(2):
                    sp.dma_start(bc_d[b, g * N:(g + 1) * N, :],
                                 ssm[R + b * N:R + (b + 1) * N, g, :]).then_inc(bc_st[g], 16)
                if g == 0:
                    sp.wait_ge(patch_mm, TT)
                    sp.wait_ge(bc_st[0], 32)
                    for r in range(2):
                        load_quad(r, r)
            for e in (E, *range(LATE[0])):
                load_expert(e)
            sp.wait_ge(bc_st[1], 32)

            with sp.Fori(0, G * Q // 2 - 1) as zz:
                for r in range(2):
                    sp.wait_ge(cs_ok, zz * (2 * IC) + IC * (r + 1))
                    load_quad(zz * 2 + (r + 2), r)
            sp.wait_ge(state_free, G * STEPS + 3)
            for e in LATE:
                load_expert(e)
            def load_rows(n, r):
                wait(sp, xs_tr, n - 1 - TT)
                sp.dma_start(xs[:, r, :], rows_v[n]).then_inc(xs_ld[r], 16)

            def store_result(n, r):
                sp.wait_ge(ysb_ok, n + 1)
                sp.dma_start(y_v[n], ysb[:, r, :]).then_inc(y_st[r], 16)

            AHEAD = 4
            for n in range(TT - AHEAD):
                store_result(n, n % 2)
            sp.wait_ge(scat_st, 16 * 2 * TT)
            for n in range(TT, TT + 2):
                load_rows(n, n % 2)
                store_result(n - AHEAD, n % 2)
            with sp.Fori(0, SLOT_TILES // 2 - 1) as j:
                for r in range(2):
                    load_rows(j * 2 + (r + TT + 2), r)
                    store_result(j * 2 + (r + TT + 2 - AHEAD), r)
            for n in range(TILES - AHEAD, TILES):
                store_result(n, n % 2)
            for r in range(2):
                sp.wait_ge(y_st[r], 16 * TT // 2)
            sp.dma_start(yg[2], y_v[0:TT].rearrange("s p d -> p s d")).then_inc(sh_ld, 16)
            sp.wait_ge(sh_ld, 16)

        def inverse_deviation(pool, chain, n):
            pool.wait_ge(aggr_ok, n + 1)
            sl = slice(TPG * (n % G), TPG * (n % G) + TPG)
            chain(pool.tensor_scalar(veps[:, sl], mv[:, sl, 1], EPS, 1.0, ALU.add, ALU.mult))
            pool.tensor_tensor(rstd[:, sl], veps[:, sl], neghalf[:, :], ALU.pow).then_inc(rstd_ok, 1)

        def scan_inputs(pool, g):
            with pool.Fori(0, Q // 2) as jj:
                for r in range(2):
                    pool.wait_ge(bc_ld[r], 32 * (Q // 2) * g + 32 + jj * 32)
                    for i in range(IC):
                        n = r * IC + i
                        pool.wait_ge(state_free, STEPS * g + n + 1 + jj * (2 * IC))
                        pool.tensor_tensor(
                            state(n % 3).rearrange("p (n t) -> p n t", n=NQ),
                            u[:, g, i, :].unsqueeze(1).to_broadcast([128, NQ, GT]),
                            bc[:, r, 0, :, :], ALU.mult).then_inc(dbu_ok, 1)

        @block.gpsimd
        def _(pool):
            link = [0]

            def chain(ins):
                link[0] += 1
                ins.then_inc(pool_c, 1)
                pool.wait_ge(pool_c, link[0])

            chain(pool.memset(ident[:, :], 0.0))
            pool.affine_select(out=ident[:, :], in_=ident[:, :], compare_op=ALU.not_equal, fill=1.0, base=0,
                               pattern=[[-1, 128]], channel_multiplier=1).then_inc(ident_ok, 1)
            pool.memset(neghalf[:, :], -0.5).then_inc(ident_ok, 1)
            chain(pool.memset(before[:, :], 1.0))
            pool.affine_select(out=before[:, :], in_=before[:, :], compare_op=ALU.is_gt, fill=0.0, base=0,
                               pattern=[[1, 128]], channel_multiplier=-1).then_inc(consts_ok, 1)
            pool.memset(ones[:, :], 1.0).then_inc(consts_ok, 1)
            pool.iota(iota_i[:, :], pattern=[[1, SLOT_TILES]], base=0, channel_multiplier=0).then_inc(consts_ok, 1)
            pool.memset(zeros[:, :], 0.0).then_inc(zero_ok, 1)
            pool.wait_ge(ident_ok, 2)
            for g in range(G):
                inverse_deviation(pool, chain, g)
            pool.wait_ge(zero_st, 16 * (SLOT_TILES // 4))
            pool.sem_inc(state_free, 3)
            for g in range(G):
                for i in range(IC):
                    pool.wait_ge(dt_ok, IC * g + i + 1)
                    pool.tensor_tensor(u[:, g, i, :], dt[:, g, i, :], h[:, g, i, :], ALU.mult).then_inc(u_ok, 1)
                pool.wait_ge(u_ok, IC * (g + 1))
                scan_inputs(pool, g)
            for g in range(G):
                inverse_deviation(pool, chain, G + g)
            pool.wait_ge(pos_ok, 1)
            for t in range(TT):
                for k in range(2):
                    pool.indirect_dma_start(
                        out=rows_d, out_offset=bass.IndirectOffsetOnAxis(ap=pos_i[:, k, t:t + 1], axis=0),
                        in_=xn[:, t, :], in_offset=None).then_inc(scat_st, 16)
            for r in range(2):
                pool.wait_ge(y_st[r], 16 * (TILES // 2))
            for t in range(TT):
                for k in range(2):
                    pool.indirect_dma_start(
                        out=yg[k][:, t, :], out_offset=None, in_=y_d,
                        in_offset=bass.IndirectOffsetOnAxis(ap=pos_i[:, k, t:t + 1], axis=0)).then_inc(gat_ld, 16)

        def transposed_to_sbuf(act, n):
            g = n % G
            act.wait_ge(xn_tr, n + 1)
            act.activation(xnTa[:, g * GT:(g + 1) * GT], ps[:, 2, :], ACT.Copy).then_inc(xnT_ok, 1)
            act.activation(xnTb[:, g * GT:(g + 1) * GT], ps[0:DB, 3, :], ACT.Copy).then_inc(xnT_ok, 1)

        @block.scalar
        def _(act):
            link = [0]

            def chain(ins):
                link[0] += 1
                ins.then_inc(act_c, 1)
                act.wait_ge(act_c, link[0])

            act.dma_start(projT[:, :, :], projT_d.rearrange("(k p) d -> p k d", p=128)).then_inc(ld_proj, 16)
            act.dma_start(projb[:, :], projb_d.partition_broadcast(128)).then_inc(ld_proj, 16)
            for half in range(2):
                act.dma_start(posb[half * S:(half + 1) * S, :], pos_d).then_inc(ld_proj, 16)
            act.dma_start(inTa[:, :], inT_d[0:DA, :]).then_inc(ld_par, 16)
            act.dma_start(inTb[:, :], inT_d[DA:D, :]).then_inc(ld_par, 16)
            act.dma_start(par[:, :, :], par_d.rearrange("(i p) n -> p i n", p=128)).then_inc(ld_par, 16)
            act.dma_start(xpT[:, :, :], xpT_d.rearrange("(i p) n -> p i n", p=128)).then_inc(ld_mid, 16)
            act.dma_start(dtT[:, :], dtT_d).then_inc(ld_mid, 16)
            act.dma_start(outT[:, :, :], outT_d.rearrange("(i p) n -> p i n", p=128)).then_inc(ld_mid, 16)
            act.dma_start(gateTa[:, :], gateT_d[0:DA, :]).then_inc(ld_mid, 16)
            act.dma_start(gateTb[:, :], gateT_d[DA:D, :]).then_inc(ld_mid, 16)
            act.wait_ge(zero_ok, 1)
            for z in range(SLOT_TILES // 4):
                act.dma_start(rows_v[TT + 4 * z:TT + 4 * z + 4].rearrange("s p d -> p s d"),
                              zeros[:, :].rearrange("p (s d) -> p s d", s=4)).then_inc(zero_st, 16)
            def conv_silu(g):
                act.wait_ge(conv_ok, g + 1)
                act.activation(h[:, g, :, :], u[:, g, :, :], ACT.Silu).then_inc(h_ok, 1)

            act.wait_ge(pads_ok, 1)
            for g in range(G):
                transposed_to_sbuf(act, g)
                for m in range(2 * IC):
                    n = 2 * IC * g + m
                    act.wait_ge(in_mm, n + 1)
                    if m < IC:
                        act.activation(hp[:, g, m, :, K - 1:],
                                       ps[:, 4 + n % 4, :].rearrange("p (b s) -> p b s", b=GB),
                                       ACT.Copy).then_inc(hidden_ok, 1)
                    else:
                        act.activation(sg[:, g, m - IC, :], ps[:, 4 + n % 4, :], ACT.Silu).then_inc(hidden_ok, 1)
                    if g == 1 and m == IC - 1:
                        conv_silu(0)
            conv_silu(1)
            act.wait_ge(ld_par, 48)
            act.wait_ge(h_ok, G)
            for g in range(G):
                for i in range(IC):
                    act.wait_ge(dt_mm, IC * g + i + 1)
                    act.activation(dt[:, g, i, :], ps[:, 1 + i, :], ACT.Identity,
                                   bias=par[:, i, P_DTB:P_DTB + 1]).then_inc(dt_lin, 1)
                act.wait_ge(dt_lin, IC * (g + 1))
                chain(act.activation(u[:, g, :, :], dt[:, g, :, :], ACT.Abs))
                chain(act.activation(u[:, g, :, :], u[:, g, :, :], ACT.Exp, scale=-1.0))
            for g in range(G):
                for i in range(IC):
                    act.activation(u[:, g, i, :], u[:, g, i, :], ACT.Ln, bias=1.0).then_inc(lnp_ok, 1)
            act.activation(negA[:, :, :], par[:, :, P_A:P_A + N], ACT.Exp).then_inc(expA_ok, 1)
            act.wait_ge(negA_ok, 1)
            for g in range(G):
                act.wait_ge(dt_ok, IC * (g + 1))
                with act.Fori(0, Q // 2) as jj:
                    for n in range(2 * IC):
                        r, i = n // IC, n % IC
                        act.wait_ge(decay_free, STEPS * g + n + 1 + jj * (2 * IC))
                        for q in range(NQ):
                            last = act.activation(
                                decay(n % 2)[:, q, :, 1:],
                                dt[:, g, i, :].rearrange("p (b s) -> p b s", b=GB)[:, :, 1:], ACT.Exp,
                                scale=negA[:, i, :].rearrange("p (j r q) -> p j r q", r=2, q=NQ)[:, jj, r, q:q + 1])
                        last.then_inc(decay_ok, 1)
            for g in range(G):
                transposed_to_sbuf(act, G + g)
            act.wait_ge(lmax_ok, 1)
            act.activation(sc[:, :, :], lg[:, :, :], ACT.Exp).then_inc(lexp_ok, 1)

            def x_copy(s, r):
                if isinstance(s, int) and s < TT:
                    return
                act.wait_ge(xs_tr, s + (1 - TT))
                act.activation(xsTa[:, r, :], ps[:, 4, 0:128], ACT.Copy)
                act.activation(xsTb[:, r, :], ps[0:DB, 4, 128:256], ACT.Copy).then_inc(xsT_ok, 1)

            def silu(s, r):
                act.wait_ge(up_a, s + 1)
                wait(act, hm_ok, s - 1)
                act.activation(sa[:, r, :], ps[:, r, :], ACT.Silu).then_inc(sa_ok, 1)

            def h_copy(s, r):
                act.wait_ge(hm_tr, s + 1)
                act.activation(hT[:, r, :, :], ps[:, 5, :].rearrange("p (c n) -> p c n", c=HC),
                               ACT.Copy).then_inc(hT_ok, 1)

            stage_loop(act, [(2, x_copy), (1, silu), (0, h_copy)])
            for t in range(TT):
                act.wait_ge(fin_ok, t + 1)
                act.dma_start(out_v[t], h0[:, t, :]).then_inc(out_st, 16)
            act.wait_ge(out_st, 16 * TT)

        @block.vector
        def _(dve):
            link = [0]

            def chain(ins):
                link[0] += 1
                ins.then_inc(dve_c, 1)
                dve.wait_ge(dve_c, link[0])

            def layer_norm(n):
                tiles = range(TPG * (n % G), TPG * (n % G) + TPG)
                for t in tiles:
                    last = dve.bn_stats(stats[:, t, :], h0[:, t, :])
                chain(last)
                for t in tiles:
                    last = dve.bn_aggr(mv[:, t, :], stats[:, t, :])
                last.then_inc(aggr_ok, 1)

            def normed(n):
                dve.wait_ge(rstd_ok, n + 1)
                for t in range(TPG * (n % G), TPG * (n % G) + TPG):
                    dve.tensor_scalar(xn[:, t, :], h0[:, t, :], mv[:, t, 0:1], rstd[:, t:t + 1],
                                      ALU.subtract, ALU.mult).then_inc(xn_ok, 1)

            dve.memset(hp[:, :, :, :, 0:K - 1].rearrange("p g i b s -> p (g i b) s"), 0.0).then_inc(pads_ok, 1)
            dve.wait_ge(ld_proj, 64)
            chain(dve.tensor_tensor(posb[:, :], posb[:, :], projb[:, :], ALU.add))
            for g in range(G):
                for t in range(TPG * g, TPG * (g + 1)):
                    dve.wait_ge(patch_mm, t + 1)
                    dve.tensor_tensor(h0[:, t, :], ps[:, t % 2, 0:D], posb[:, :], ALU.add).then_inc(h0_ok, 1)
                if g:
                    normed(0)
                dve.wait_ge(h0_ok, TPG * (g + 1))
                layer_norm(g)
            normed(1)
            dve.wait_ge(consts_ok, 3)
            chain(dve.tensor_copy(iota[:, :], iota_i[:, :]))
            dve.tensor_scalar(steps[:, :], iota[:, 0:TT], 128.0, None, ALU.mult)
            dve.wait_ge(ld_par, 48)
            def scan_coefficients(g):
                dve.wait_ge(xp_mm, g + 1)
                dve.tensor_copy(ssm[:, g, :], ps[0:R + 2 * N, 0, :]).then_inc(ssm_ok, 1)

            for g in range(G):
                for i in range(IC):
                    dve.wait_ge(hidden_ok, 2 * IC * g + i + 1)
                    out = u[:, g, i, :].rearrange("p (b s) -> p b s", b=GB)
                    chain(dve.tensor_scalar(out, hp[:, g, i, :, 0:S], par[:, i, P_CW:P_CW + 1],
                                            par[:, i, P_CB:P_CB + 1], ALU.mult, ALU.add))
                    for k in range(1, K):
                        ins = dve.scalar_tensor_tensor(out, hp[:, g, i, :, k:k + S], par[:, i, P_CW + k:P_CW + k + 1],
                                                       out, ALU.mult, ALU.add)
                        if i == IC - 1 and k == K - 1:
                            ins.then_inc(conv_ok, 1)
                        else:
                            chain(ins)
                if g == 0:
                    dve.wait_ge(ident_ok, 2)
            scan_coefficients(0)
            dve.wait_ge(conv_ok, G)
            for r in range(2):
                dve.memset(decay(r)[:, :, :, 0:1].rearrange("p n b s -> p (n b) s"), 0.0).then_inc(decay_free, 1)
            for i in range(IC):
                dve.tensor_scalar(diagD[:, i, :], ident[:, :], par[:, i, P_D:P_D + 1], None, ALU.mult).then_inc(diag_ok, 1)
            scan_coefficients(1)
            for g in range(G):
                for i in range(IC):
                    dve.wait_ge(lnp_ok, IC * g + i + 1)
                    chain(dve.scalar_tensor_tensor(dt[:, g, i, :], dt[:, g, i, :], 0.0, u[:, g, i, :],
                                                   ALU.max, ALU.add))
                    end = dt[:, g, i, S - 1::S]
                    dve.tensor_scalar(end, end, par[:, i, P_ALPHA:P_ALPHA + 1], None, ALU.mult).then_inc(dt_ok, 1)
            dve.wait_ge(expA_ok, 1)
            dve.tensor_scalar(negA[:, :, :], negA[:, :, :], -1.0, None, ALU.mult).then_inc(negA_ok, 1)
            for g in range(G):
                with dve.Fori(0, Q // 2) as jj:
                    for n in range(2 * IC):
                        r, i = n // IC, n % IC
                        s = STEPS * g + n
                        dve.wait_ge(decay_ok, s + 1 + jj * (2 * IC))
                        dve.wait_ge(dbu_ok, s + 1 + jj * (2 * IC))
                        dve.tensor_tensor_scan(state(n % 3), ring[:, n % 2, :], state(n % 3), 0.0,
                                               ALU.mult, ALU.add).then_inc(decay_free, 1)
                        dve.wait_ge(decay_free, s + 3 + jj * (2 * IC))
                        dve.tensor_tensor(state(n % 3), state(n % 3),
                                          bc[:, r, 1, :, :].rearrange("p n t -> p (n t)"),
                                          ALU.mult).then_inc(cs_ok, 1)
            dve.wait_ge(hidden_ok, 2 * IC * G)
            for g in range(G):
                dve.wait_ge(state_free, STEPS * (g + 1) + 3)
                for i in range(IC):
                    dve.tensor_tensor(sg[:, g, i, :], ps[:, YBANK[g] + i, :], sg[:, g, i, :], ALU.mult).then_inc(yevac, 1)
                dve.wait_ge(yevac, IC * (g + 1))
                for i in range(IC):
                    end = sg[:, g, i, S - 1::S]
                    dve.tensor_scalar(end, end, par[:, i, P_FG:P_FG + 1], None, ALU.mult).then_inc(y_ok, 1)
            dve.wait_ge(xn_tr, G)
            for g in range(G):
                for t in range(TPG * g, TPG * (g + 1)):
                    dve.wait_ge(op_mm, t + 1)
                    dve.tensor_tensor(h0[:, t, :], ps[:, OBANK[t % 2], 0:D], h0[:, t, :], ALU.add).then_inc(h1_ok, 1)
                if g:
                    normed(G)
                dve.wait_ge(h1_ok, TPG * (g + 1))
                layer_norm(G + g)
            normed(G + 1)
            def over_e(ap):
                return ap.unsqueeze(2).to_broadcast([128, TT, E])

            dve.wait_ge(lg_mm, 1)
            chain(dve.tensor_copy(lg[:, :, :], ps[:, 7, 0:TT * E].rearrange("p (t e) -> p t e", t=TT)))
            chain(dve.tensor_reduce(red[:, 0, :], lg[:, :, :], AX.X, ALU.max))
            dve.tensor_tensor(lg[:, :, :], lg[:, :, :], over_e(red[:, 0, :]), ALU.subtract).then_inc(lmax_ok, 1)
            dve.wait_ge(lexp_ok, 1)
            chain(dve.tensor_reduce(red[:, 1, :], sc[:, :, :], AX.X, ALU.add))
            chain(dve.reciprocal(red[:, 1, :], red[:, 1, :]))
            chain(dve.tensor_tensor(sc[:, :, :], sc[:, :, :], over_e(red[:, 1, :]), ALU.mult))
            for t in range(TT):
                last = dve.max(m8[:, t, :], sc[:, t, :])
            chain(last)
            for t in range(TT):
                last = dve.max_index(ix[:, t, :], m8[:, t, :], sc[:, t, :])
            chain(last)
            for k in range(2):
                last = dve.tensor_copy(ixf[:, k, :], ix[:, :, k])
            chain(last)
            for k in range(2):
                last = dve.tensor_tensor(hot[:, k, :, :], iota[:, 0:E].unsqueeze(1).to_broadcast([128, TT, E]),
                                         over_e(ixf[:, k, :]), ALU.is_equal)
            chain(last)
            dve.memset(mcum[:, 0, :], 0.0)
            chain(dve.tensor_tensor(msum[:, :, :], hot[:, 0, :, :], hot[:, 1, :, :], ALU.add))
            for t in range(TT):
                ins = dve.tensor_tensor(mcum[:, t + 1, :], mcum[:, t, :], msum[:, t, :], ALU.add)
                if t < TT - 1:
                    chain(ins)
                else:
                    ins.then_inc(mcum_ok, 1)
            chain(dve.tensor_tensor(red[:, 2, :], m8[:, :, 0], m8[:, :, 1], ALU.add))
            chain(dve.tensor_scalar(red[:, 2, :], red[:, 2, :], 1e-20, None, ALU.add))
            chain(dve.reciprocal(red[:, 2, :], red[:, 2, :]))
            for k in range(2):
                last = dve.tensor_tensor(wk[:, k, :], m8[:, :, k], red[:, 2, :], ALU.mult)
            chain(last)
            dve.wait_ge(rank_mm, 1)
            dve.tensor_copy(rank[:, :, :], ps[:, 7, 128:128 + TT * E].rearrange("p (t e) -> p t e", t=TT))
            chain(dve.tensor_copy(cnt[:, :], ps[:, 7, 128 + TT * E:128 + (TT + 1) * E]))
            gt_v = gt[:, :].rearrange("p (e k) -> p e k", k=TT)
            chain(dve.tensor_tensor(gt_v, cnt[:, :].unsqueeze(2).to_broadcast([128, E, TT]),
                                    steps[:, :].unsqueeze(1).to_broadcast([128, E, TT]), ALU.is_gt))
            chain(dve.tensor_reduce(ntile[:, :], gt_v, AX.X, ALU.add))
            chain(dve.tensor_tensor_scan(tend[:, :], ones[:, 0:E], ntile[:, :], 0.0, ALU.mult, ALU.add))
            chain(dve.tensor_tensor(base[:, :], tend[:, :], ntile[:, :], ALU.subtract))
            chain(dve.tensor_scalar(base[:, :], base[:, :], float(TT), 128.0, ALU.add, ALU.mult))
            chain(dve.tensor_tensor(rank[:, :, :], rank[:, :, :],
                                    base[:, :].unsqueeze(1).to_broadcast([128, TT, E]), ALU.add))
            for k in range(2):
                last = dve.tensor_tensor(hot[:, k, :, :], hot[:, k, :, :], rank[:, :, :], ALU.mult)
            chain(last)
            chain(dve.tensor_reduce(posf[:, :, :], hot[:, :, :, :], AX.X, ALU.add))
            dve.tensor_copy(pos_i[:, :, :], posf[:, :, :]).then_inc(pos_ok, 1)
            chain(dve.tensor_tensor(tcmp[:, :, :], iota[:, :].unsqueeze(2).to_broadcast([128, SLOT_TILES, E]),
                                    tend[:, :].unsqueeze(1).to_broadcast([128, SLOT_TILES, E]), ALU.is_ge))
            dve.memset(tef[:, 0:TT], float(E))
            chain(dve.tensor_reduce(tef[:, TT:], tcmp[:, :, :], AX.X, ALU.add))
            chain(dve.tensor_scalar(tef[:, TT:], tef[:, TT:], float(E - 1), None, ALU.min))
            dve.tensor_copy(te[:, :], tef[:, :]).then_inc(te_ok, 1)

            def gated(s, r):
                dve.wait_ge(up_c, s + 1)
                dve.wait_ge(sa_ok, s + 1)
                dve.tensor_tensor(hm[:, r, :], ps[:, 2 + r, :], sa[:, r, :], ALU.mult).then_inc(hm_ok, 1)

            def result(s, r):
                dve.wait_ge(down_mm, s + 1)
                if isinstance(s, int):
                    wait(dve, y_st[r], 16 * (s // 2))
                else:
                    dve.wait_ge(y_st[r], s * 8 - 8 * r)
                dve.tensor_copy(ysb[:, r, :], ps[:, 6 + r, 0:D]).then_inc(ysb_ok, 1)

            stage_loop(dve, [(1, gated), (-1, result)])
            dve.wait_ge(sh_ld, 16)
            chain(dve.tensor_tensor(h0[:, :, :], h0[:, :, :], yg[2], ALU.add))
            dve.wait_ge(gat_ld, 16 * 2 * TT)
            for t in range(TT):
                last = dve.scalar_tensor_tensor(h0[:, t, :], yg[0][:, t, :], wk[:, 0, t:t + 1], h0[:, t, :],
                                                ALU.mult, ALU.add)
            chain(last)
            for t in range(TT):
                dve.scalar_tensor_tensor(h0[:, t, :], yg[1][:, t, :], wk[:, 1, t:t + 1], h0[:, t, :],
                                         ALU.mult, ALU.add).then_inc(fin_ok, 1)

        @block.tensor
        def _(pe):
            def transposes(n):
                g = n % G
                pe.wait_ge(xn_ok, TPG * (n + 1))
                if n:
                    pe.wait_ge(xnT_ok, 2 * n)
                for q in range(TPG):
                    t = TPG * g + q
                    pe.transpose(ps[:, 2, 128 * q:128 * (q + 1)], xn[:, t, 0:DA], ident[:, :])
                    last = pe.transpose(ps[0:DB, 3, 128 * q:128 * (q + 1)], xn[:, t, DA:D], ident[:, :])
                last.then_inc(xn_tr, 1)

            pe.wait_ge(ld_proj, 64)
            for t in range(TT):
                if t % TPG == 0:
                    pe.wait_ge(ld_x[t // TPG], 16)
                if t >= 2:
                    pe.wait_ge(h0_ok, t - 1)
                for k in range(PK):
                    last = pe.matmul(ps[:, t % 2, 0:D], xT[:, k, 128 * t:128 * (t + 1)], projT[:, k, :],
                                     start=(k == 0), stop=(k == PK - 1))
                last.then_inc(patch_mm, 1)
            pe.wait_ge(ident_ok, 2)
            for g in range(G):
                transposes(g)
                pe.wait_ge(xnT_ok, 2 * (g + 1))
                if g == 0:
                    pe.wait_ge(ld_par, 48)
                for m in range(2 * IC):
                    n = 2 * IC * g + m
                    if n >= 4:
                        pe.wait_ge(hidden_ok, n - 3)
                    pe.matmul(ps[:, 4 + n % 4, :], inTa[:, 128 * m:128 * (m + 1)], xnTa[:, GT * g:GT * (g + 1)],
                              start=True, stop=False)
                    pe.matmul(ps[:, 4 + n % 4, :], inTb[:, 128 * m:128 * (m + 1)], xnTb[:, GT * g:GT * (g + 1)],
                              start=False, stop=True).then_inc(in_mm, 1)
            pe.wait_ge(ld_mid, 80)
            pe.wait_ge(h0_ok, TT)
            pe.wait_ge(xnT_ok, 2 * G)
            for g in range(G):
                pe.wait_ge(h_ok, g + 1)
                for i in range(IC):
                    last = pe.matmul(ps[0:R + 2 * N, 0, :], xpT[:, i, :], h[:, g, i, :], start=(i == 0), stop=(i == IC - 1))
                last.then_inc(xp_mm, 1)
                pe.wait_ge(ssm_ok, g + 1)
                if g:
                    pe.wait_ge(dt_lin, IC * g)
                for i in range(IC):
                    pe.matmul(ps[:, 1 + i, :], dtT[:, 128 * i:128 * (i + 1)], ssm[0:R, g, :],
                              start=True, stop=True).then_inc(dt_mm, 1)
            pe.wait_ge(diag_ok, IC)
            for g in range(G):
                pe.wait_ge(*((hidden_ok, 2 * IC * G), (dt_lin, IC * G))[g])
                for i in range(IC):
                    pe.matmul(ps[:, YBANK[g] + i, :], diagD[:, i, :], h[:, g, i, :], start=True, stop=True)
                with pe.Fori(0, Q // 2) as jj:
                    for n in range(2 * IC):
                        pe.wait_ge(cs_ok, STEPS * g + n + 1 + jj * (2 * IC))
                        for q in range(NQ):
                            last = pe.matmul(ps[:, YBANK[g] + n % IC, :], ident[:, :], state(n % 3)[:, q * GT:(q + 1) * GT],
                                             start=False, stop=True, skip_group_check=True)
                        last.then_inc(state_free, 1)
            for t in range(TT):
                g, q = t // TPG, t % TPG
                if q == 0:
                    pe.wait_ge(y_ok, IC * (g + 1))
                if t >= 2:
                    pe.wait_ge(h1_ok, t - 1)
                for i in range(IC):
                    last = pe.matmul(ps[:, OBANK[t % 2], 0:D], sg[:, g, i, 128 * q:128 * (q + 1)], outT[:, i, :],
                                     start=(i == 0), stop=(i == IC - 1))
                last.then_inc(op_mm, 1)
            for g in range(G):
                transposes(G + g)
            pe.wait_ge(h1_ok, TT)
            pe.wait_ge(xnT_ok, 4 * G)
            for t in range(TT):
                o = ps[:, 7, t * E:(t + 1) * E]
                pe.matmul(o, xnTa[:, 128 * t:128 * (t + 1)], gateTa[:, :], start=True, stop=False)
                last = pe.matmul(o, xnTb[:, 128 * t:128 * (t + 1)], gateTb[:, :], start=False, stop=True)
            last.then_inc(lg_mm, 1)
            pe.wait_ge(mcum_ok, 1)
            pe.wait_ge(consts_ok, 3)
            o = ps[:, 7, 128:128 + (TT + 1) * E]
            pe.matmul(o, ones[:, :], mcum[:, :, :].rearrange("p t e -> p (t e)"), start=True, stop=True)
            pe.matmul(o[:, 0:TT * E], before[:, :], msum[:, :, :].rearrange("p t e -> p (t e)"),
                      start=False, stop=True, skip_group_check=True).then_inc(rank_mm, 1)

            def x_transposes(s, r):
                if isinstance(s, int) and s < TT:
                    return
                pe.wait_ge(xs_ld[r], s * 8 + (16 - 8 * r - 8 * TT))
                wait(pe, xsT_ok, s - TT)
                pe.transpose(ps[:, 4, 0:128], xs[:, r, 0:DA], ident[:, :])
                pe.transpose(ps[0:DB, 4, 128:256], xs[:, r, DA:D], ident[:, :]).then_inc(xs_tr, 1)

            routed = [False]

            def expert(s):
                if not routed[0]:
                    return E
                return pe.value_load(te[0:1, s:s + 1] if isinstance(s, int) else te[0:1, bass.ds(s, 1)],
                                     min_val=0, max_val=E)

            def up(s, r):
                e = expert(s)
                if isinstance(s, int) and s < TT:
                    xa, xb = xnTa[:, 128 * s:128 * (s + 1)], xnTb[:, 128 * s:128 * (s + 1)]
                else:
                    pe.wait_ge(xsT_ok, s + (1 - TT))
                    xa, xb = xsTa[:, r, :], xsTb[:, r, :]
                wait(pe, hm_ok, s - 1)
                for c, done in ((0, up_a), (1, up_c)):
                    o = ps[:, 2 * c + r, :]
                    pe.matmul(o, xa, w13a[:, e, c * HID:(c + 1) * HID], start=True, stop=False)
                    pe.matmul(o, xb, w13b[:, e, c * HID:(c + 1) * HID], start=False, stop=True).then_inc(done, 1)

            def h_transposes(s, r):
                pe.wait_ge(hm_ok, s + 1)
                wait(pe, hT_ok, s)
                for c in range(HC):
                    last = pe.transpose(ps[:, 5, 128 * c:128 * (c + 1)], hm[:, r, 128 * c:128 * (c + 1)], ident[:, :])
                last.then_inc(hm_tr, 1)

            def down(s, r):
                e = expert(s)
                pe.wait_ge(hT_ok, s + 1)
                wait(pe, ysb_ok, s - 1)
                for c in range(HC):
                    last = pe.matmul(ps[:, 6 + r, 0:D], hT[:, r, c, :], w2[:, e, c * D:(c + 1) * D],
                                     start=(c == 0), stop=(c == HC - 1))
                last.then_inc(down_mm, 1)

            def routed_ready():
                pe.wait_ge(te_ok, 1)
                pe.wait_ge(ld_w, 16 * 3 * (E + 1))
                routed[0] = True

            pe.wait_ge(ld_w, 16 * 3 * (LATE[0] + 1))
            stage_loop(pe, [(2, x_transposes), (1, up), (0, h_transposes), (-1, down)], routed_ready)


_ARRAYS = ("xT", "projT", "projb", "pos", "inT", "params", "xpT", "dtT", "outT", "gateT", "w13T", "w2T")


def kernel(x, L0_tok_proj_w, L0_tok_proj_b, L0_tok_pos_emb, L0_attn_in_proj_w, L0_attn_conv_w, L0_attn_conv_b,
           L0_attn_x_proj_w, L0_attn_dt_proj_w, L0_attn_dt_proj_b, L0_attn_A_log, L0_attn_D, L0_attn_out_proj_w,
           L0_attn_alpha, L0_attn_feature_gating, L0_ffn_gate_w, L0_ffn_w1, L0_ffn_w2, L0_ffn_w3,
           L0_ffn_ws1, L0_ffn_ws2, L0_ffn_ws3):
    import concourse.bacc as bacc
    from concourse.bass_utils import run_bass_kernel_spmd

    a = np.asarray
    col = lambda v: a(v).reshape(I, 1)
    side = IMG // PATCH
    w1 = np.concatenate([a(L0_ffn_w1), a(L0_ffn_ws1)[None]]).transpose(0, 2, 1)
    w3 = np.concatenate([a(L0_ffn_w3), a(L0_ffn_ws3)[None]]).transpose(0, 2, 1)
    laid = {
        "xT": (a(x).reshape(B, C_IN, side, PATCH, side, PATCH).transpose(0, 1, 2, 4, 3, 5)
               .reshape(T, PD).T),
        "projT": a(L0_tok_proj_w).T,
        "projb": a(L0_tok_proj_b),
        "pos": a(L0_tok_pos_emb)[0],
        "inT": a(L0_attn_in_proj_w).T,
        "params": np.concatenate([a(L0_attn_conv_w)[:, 0], col(L0_attn_conv_b), col(L0_attn_dt_proj_b),
                                  a(L0_attn_A_log), col(L0_attn_D), col(L0_attn_alpha),
                                  col(L0_attn_feature_gating)], axis=1),
        "xpT": a(L0_attn_x_proj_w).T,
        "dtT": a(L0_attn_dt_proj_w).T,
        "outT": a(L0_attn_out_proj_w).T,
        "gateT": a(L0_ffn_gate_w).T,
        "w13T": np.concatenate([w1, w3], axis=2),
        "w2T": np.concatenate([a(L0_ffn_w2), a(L0_ffn_ws2)[None]]).transpose(0, 2, 1),
    }
    laid = {n: np.ascontiguousarray(v) for n, v in laid.items()}
    nc = bacc.Bacc("TRN2", target_bir_lowering=False, num_devices=1)
    args = [nc.dram_tensor("in_" + n, laid[n].shape, F32, kind="ExternalInput").ap() for n in _ARRAYS]
    out = nc.dram_tensor("out", (T, D), F32, kind="ExternalOutput").ap()
    program(nc, *args, out)
    r = run_bass_kernel_spmd(nc, [{"in_" + n: v for n, v in laid.items()}], core_ids=[0])
    return r.results[0]["out"].reshape(B, S, D)
```

```python
import numpy as np
import concourse.bass as bass
import concourse.mybir as mybir
from concourse.alu_op_type import AluOpType as ALU
from contextlib import ExitStack

F32 = mybir.dt.float32
F32R = mybir.dt.float32r
I32 = mybir.dt.int32
U32 = mybir.dt.uint32
ACT = mybir.ActivationFunctionType
AX = mybir.AxisListType

B, C_IN, IMG, PATCH = 16, 2, 128, 16
S = (IMG // PATCH) ** 2
D = 192
DA, DB = 128, D - 128
PD = C_IN * PATCH * PATCH
PK = PD // 128
T = B * S
TT = T // 128
G = 2
GT = T // G
GB = B // G
TPG = TT // G
I = 384
IC = I // 128
N = 16
R = 48
K = 4
NQ = 4
Q = N // NQ
E = 8
HID = 512
HC = HID // 128
SLOT_TILES = (2 * T + E * 127) // 128
TILES = TT + SLOT_TILES
ROW = 2 * DA + 4
FIRST_EXPERT, WEIGHT, TOKEN = 2 * DA, 2 * DA + 1, 2 * DA + 3
EPS = 1e-5
PARAMS = K + 1 + 1 + N + 1 + 1 + 1
P_CW, P_CB, P_DTB, P_A, P_D, P_ALPHA, P_FG = 0, K, K + 1, K + 2, K + 2 + N, K + 3 + N, K + 4 + N


def program(nc, xT_d, projT_d, projb_d, pos_d, inT_d, par_d, xpT_d, dtT_d, outT_d, gateT_d, w13T_d, w2T_d, out_d):
    ctx = ExitStack()
    with ctx:
        def sb(name, shape, dt=F32):
            return ctx.enter_context(nc.sbuf_tensor(name, shape, dt))

        def sem(name):
            return ctx.enter_context(nc.semaphore(name))

        bc_d = nc.dram_tensor("bc_scratch", [2, G * N, GT], F32).ap()
        rows_d = nc.dram_tensor("rows_scratch", [SLOT_TILES * 128, ROW], F32).ap()
        sum_d = nc.dram_tensor("sum_scratch", [T + 128, D], F32).ap()

        STAGE = 3
        front_at = -(-nc.sbuf_base // 32) * 32
        sb("front_memory", [128, 3584])
        at = [front_at]

        def place(name, shape, dt=F32):
            size = -(-4 * int(np.prod(shape[1:])) // 32) * 32
            t = nc.alloc_sbuf_tensor_at(name, shape, dt, offset=at[0])
            at[0] += size
            return t

        projT = place("projT", [128, PK, D])
        inTa = place("inTa", [DA, 2 * I])
        inTb = place("inTb", [DB, 2 * I])
        xpT = place("xpT", [128, IC, R + 2 * N])
        dtT = place("dtT", [R, I])
        posb = place("posb", [128, D])
        projb = place("projb", [128, D])
        assert at[0] <= front_at + 4 * 3584
        at[0] = front_at
        raw = place("raw", [128, STAGE, 2 * HID])
        W13 = 3 * 2 * HID
        scan_at = -(-nc.sbuf_base // 32) * 32
        sb("scan_memory", [128, (E + 1) * W13])
        at[0] = scan_at
        h = place("h", [128, G, IC, GT])
        dt = place("dt", [128, G, IC, GT])
        u = place("u", [128, G, IC, GT])
        decays = place("decays", [128, 2, NQ * GT])
        states = place("states", [128, 3, NQ * GT])
        bc = place("bc", [128, 2, 2, NQ, GT])
        assert at[0] <= scan_at + 4 * (E + 1) * W13
        at[0] = scan_at
        w13 = place("w13", [128, E + 1, 3, 2 * HID], F32R)
        par = sb("par", [128, IC, PARAMS])
        negA = sb("negA", [128, IC, N])
        diagD = sb("diagD", [128, IC, 128])
        outT = sb("outT", [128, IC, D])
        gateTa = sb("gateTa", [DA, E])
        gateTb = sb("gateTb", [DB, E])
        w2_at = -(-nc.sbuf_base // 32) * 32
        w2 = sb("w2", [128, E + 1, HC * D])
        ident = sb("ident", [128, 128])
        ones = sb("ones", [128, 128])
        before = sb("before", [128, 128])
        iota_i = sb("iota_i", [128, SLOT_TILES], I32)
        iota = sb("iota", [128, SLOT_TILES])
        steps = sb("steps", [128, TT])
        neghalf = sb("neghalf", [128, TPG])
        h0 = sb("h0", [128, TT, D])
        xn = sb("xn", [128, TT, ROW])
        stats = sb("stats", [128, TT, 6])
        mv = sb("mv", [128, TT, 2])
        veps = sb("veps", [128, TT])
        rstd = sb("rstd", [128, TT])
        xnT = sb("xnT", [128, 2, T])
        ssm = sb("ssm", [R + 2 * N, G, GT])
        sg_at = -(-nc.sbuf_base // 32) * 32
        sg = sb("sg", [128, G, IC, GT])
        lg = sb("lg", [128, TT, E])
        sc = sb("sc", [128, TT, E])
        red = sb("red", [128, 4, TT])
        m8 = sb("m8", [128, TT, 8])
        ix = sb("ix", [128, TT, 8], U32)
        ixf = sb("ixf", [128, 2, TT])
        hot = sb("hot", [128, 2, TT, E])
        msum = sb("msum", [128, TT, E])
        mcum = sb("mcum", [128, TT + 1, E])
        rank = sb("rank", [128, TT, E])
        cnt = sb("cnt", [128, E])
        gt = sb("gt", [128, E * TT])
        ntile = sb("ntile", [128, E])
        tend = sb("tend", [128, E])
        base = sb("base", [128, E])
        posf = sb("posf", [128, 2, TT])
        pos_i = sb("pos_i", [128, 2, TT], I32)
        tcmp = sb("tcmp", [128, SLOT_TILES, E])
        tef = sb("tef", [128, SLOT_TILES])
        te = sb("te", [128, SLOT_TILES], I32)
        token_i = sb("token_i", [128, TT + 1], I32)
        info = sb("info", [128, SLOT_TILES, ROW - 2 * DA])
        chosen = sb("chosen", [128, 2, SLOT_TILES])
        weight = sb("weight", [128, SLOT_TILES])
        token = sb("token", [128, SLOT_TILES], I32)
        token_r = sb("token_r", [128, 2], I32)
        xs = sb("xs", [128, 2, 2 * DA])
        xs_high = sb("xs_high", [128, 2, 2, 128], F32R)
        xs_low = sb("xs_low", [128, 2, 2, 128], F32R)
        ysb = sb("ysb", [128, 2, D])
        at[0] = sg_at
        sa = place("sa", [128, 2, HID])
        hm = place("hm", [128, 2, HID])
        hT = place("hT", [128, 2, HC, 128])
        assert at[0] <= sg_at + 4 * G * IC * GT
        xT = bc[:, :, :, :, :].rearrange("p a b q t -> p (a b q t)")[:, 0:PK * T].rearrange("p (k t) -> p k t", k=PK)
        hp = decays[:, :, :].rearrange("p r n -> p (r n)")[:, 0:G * IC * GB * (S + K - 1)].rearrange(
            "p (g i b s) -> p g i b s", g=G, i=IC, b=GB)
        zeros = states[:, 0, 0:4 * ROW].rearrange("p (s d) -> p s d", s=4)

        ps = ctx.enter_context(nc.psum_tensor("ps", [128, 8, 512], F32))

        def decay(r):
            return decays[:, r, :].rearrange("p (n b s) -> p n b s", n=NQ, b=GB)

        def state(r):
            return states[:, r, :]

        ld_x = [sem(f"ld_x{g}") for g in range(G)]
        ld_proj = sem("ld_proj")
        ld_par = sem("ld_par")
        ld_mid = sem("ld_mid")
        ld_w2 = sem("ld_w2")
        raw_ld = [sem(f"raw_ld{r}") for r in range(STAGE)]
        high_ok = sem("high_ok")
        low_ok = sem("low_ok")
        ident_ok = sem("ident_ok")
        pool_c = sem("pool_c")
        dve_c = sem("dve_c")
        act_c = sem("act_c")
        consts_ok = sem("consts_ok")
        patch_mm = sem("patch_mm")
        h0_ok = sem("h0_ok")
        aggr_ok = sem("aggr_ok")
        rstd_ok = sem("rstd_ok")
        xn_ok = sem("xn_ok")
        xn_tr = sem("xn_tr")
        xnT_ok = sem("xnT_ok")
        in_mm = sem("in_mm")
        in_used = sem("in_used")
        pads_ok = sem("pads_ok")
        hidden_ok = sem("hidden_ok")
        conv_ok = sem("conv_ok")
        h_ok = sem("h_ok")
        xp_mm = sem("xp_mm")
        ssm_ok = sem("ssm_ok")
        bc_st = [sem(f"bc_st{g}") for g in range(G)]
        bc_ld = [sem(f"bc_ld{r}") for r in range(2)]
        dt_mm = sem("dt_mm")
        dt_lin = sem("dt_lin")
        lnp_ok = sem("lnp_ok")
        expA_ok = sem("expA_ok")
        negA_ok = sem("negA_ok")
        diag_ok = sem("diag_ok")
        dt_ok = sem("dt_ok")
        u_ok = sem("u_ok")
        decay_free = sem("decay_free")
        state_free = sem("state_free")
        decay_ok = sem("decay_ok")
        dbu_ok = sem("dbu_ok")
        cs_ok = sem("cs_ok")
        yevac = sem("yevac")
        y_ok = sem("y_ok")
        op_mm = sem("op_mm")
        h1_ok = sem("h1_ok")
        zero_ok = sem("zero_ok")
        zero_st = sem("zero_st")
        ids_ok = sem("ids_ok")
        lg_mm = sem("lg_mm")
        lmax_ok = sem("lmax_ok")
        lexp_ok = sem("lexp_ok")
        mcum_ok = sem("mcum_ok")
        rank_mm = sem("rank_mm")
        pos_ok = sem("pos_ok")
        te_ok = sem("te_ok")
        scat_st = sem("scat_st")
        xs_ld = [sem(f"xs_ld{r}") for r in range(2)]
        xs_tr = sem("xs_tr")
        x_high_ok = sem("x_high_ok")
        x_low_ok = sem("x_low_ok")
        up_a = sem("up_a")
        up_c = sem("up_c")
        sa_ok = sem("sa_ok")
        hm_ok = sem("hm_ok")
        hm_tr = sem("hm_tr")
        hT_ok = sem("hT_ok")
        down_mm = sem("down_mm")
        ysb_ok = sem("ysb_ok")
        y_st = [sem(f"y_st{r}") for r in range(2)]
        info_ld = sem("info_ld")
        slots_ok = sem("slots_ok")
        token_ok = sem("token_ok")
        add_start = sem("add_start")
        spare_st = sem("spare_st")
        sum_st = sem("sum_st")
        out_st = sem("out_st")

        STEPS = Q * IC
        YBANK = (4, 1)
        OBANK = (0, 7)
        rows_v = rows_d.rearrange("(s p) d -> s p d", p=128)
        sum_v = sum_d.rearrange("(s p) d -> s p d", p=128)

        HALVES = [(e, half) for e in range(E + 1) for half in range(2)]

        IN_H_DT, IN_U, BEFORE_SCATTER = 4, 6, 8

        def late_halves(s):
            first = BEFORE_SCATTER + 2 * (s - 2)
            return range(max(first, BEFORE_SCATTER), min(first + 2, len(HALVES)))

        def high_part(act, v):
            e, half = HALVES[v]
            act.wait_ge(raw_ld[v % STAGE], raw_count(v))
            act.activation(w13[:, e, 2 * half, :], raw[:, v % STAGE, :], ACT.Copy).then_inc(high_ok, 1)

        def raw_count(v):
            return 16 * sum(1 + HALVES[x][1] for x in range(v % STAGE, v + 1, STAGE))

        def low_part(eng, v):
            e, half = HALVES[v]
            eng.wait_ge(high_ok, v + 1)
            wait(eng, low_ok, v)
            rows = slice(DB * half, 128)
            eng.tensor_tensor(w13[rows, e, 1 + half, :], raw[rows, v % STAGE, :],
                              w13[rows, e, 2 * half, :].bitcast(F32), ALU.subtract).then_inc(low_ok, 1)

        def wait(eng, signal, count):
            if not isinstance(count, int) or count > 0:
                eng.wait_ge(signal, count)

        block = ctx.enter_context(nc.Block())

        LOOP_START = TT + 5
        assert (TILES - 2 - LOOP_START) % 2 == 0

        def stage_loop(eng, parts, between=None):
            def step(s, r, ends):
                for lag, part in parts:
                    if not ends or 0 <= s + lag < TILES:
                        part(s + lag, (r + lag) % 2)

            for s in range(-2, LOOP_START):
                if between:
                    between(s)
                step(s, s % 2, True)
            with eng.Fori(0, (TILES - 2 - LOOP_START) // 2) as j:
                for s in range(LOOP_START, LOOP_START + 2):
                    step(j * 2 + s, s % 2, False)
            for s in range(TILES - 2, TILES + 1):
                step(s, s % 2, True)

        @block.sync
        def _(sp):
            xT_v = xT_d.rearrange("(k p) t -> p k t", p=128)
            sp.dma_start(xT[:, :, 0:GT], xT_v[:, :, 0:GT]).then_inc(ld_x[0], 16)
            sp.dma_start(xT[:, :, GT:T], xT_v[:, :, GT:T]).then_inc(ld_x[1], 16)
            def load_half(v):
                e, half = HALVES[v]
                wait(sp, low_ok, v - STAGE + 1)
                if half == 0:
                    sp.dma_start(raw[:, v % STAGE, :], w13T_d[e, 0:DA, :]).then_inc(raw_ld[v % STAGE], 16)
                else:
                    for rows in (slice(0, DB), slice(DB, 128)):
                        sp.dma_start(raw[rows, v % STAGE, :], w13T_d[e, DA:D, :]).then_inc(raw_ld[v % STAGE], 16)

            def load_quad(z, r):
                for b in range(2):
                    sp.dma_start(bc[:, r, b, :, :],
                                 bc_d[b].rearrange("(z q) t -> z q t", q=NQ)[z].partition_broadcast(128)
                                 ).then_inc(bc_ld[r], 16)

            for g in range(G):
                sp.wait_ge(ssm_ok, g + 1)
                for b in range(2):
                    sp.dma_start(bc_d[b, g * N:(g + 1) * N, :],
                                 ssm[R + b * N:R + (b + 1) * N, g, :]).then_inc(bc_st[g], 16)
                if g == 0:
                    sp.wait_ge(patch_mm, TT)
                    sp.wait_ge(bc_st[0], 32)
                    for r in range(2):
                        load_quad(r, r)
            for e in range(E + 1):
                sp.dma_start(w2[:, e, :].rearrange("p (c d) -> p c d", c=HC),
                             w2T_d[e].rearrange("(c p) d -> p c d", p=128)).then_inc(ld_w2, 16)
            sp.wait_ge(dt_lin, IC * G)
            for v in range(STAGE):
                load_half(v)
            sp.wait_ge(bc_st[1], 32)

            with sp.Fori(0, G * Q // 2 - 1) as zz:
                for r in range(2):
                    sp.wait_ge(cs_ok, zz * (2 * IC) + IC * (r + 1))
                    load_quad(zz * 2 + (r + 2), r)
            for v in range(STAGE, BEFORE_SCATTER + STAGE):
                load_half(v)

            def load_rows(n, r):
                wait(sp, xs_tr, n - 1)
                sp.dma_start(xs[:, r, :], rows_v[n][:, 0:2 * DA]).then_inc(xs_ld[r], 16)

            def store_shared(n):
                sp.wait_ge(ysb_ok, n + 1)
                sp.dma_start(sum_v[n], ysb[:, n % 2, :]).then_inc(y_st[n % 2], 16)

            EARLY = TT // 2 + 1
            for n in range(EARLY):
                for v in late_halves(n + 1):
                    if v + STAGE < len(HALVES):
                        load_half(v + STAGE)
                store_shared(n)
            sp.wait_ge(scat_st, 16 * 2 * TT)
            for n in range(2):
                load_rows(n, n)
            sp.dma_start(info[:, :, :], rows_v[:, :, 2 * DA:].rearrange("s p d -> p s d")).then_inc(info_ld, 16)
            for n in range(EARLY, TT - 1):
                store_shared(n)
            for n in range(2, 4):
                load_rows(n, n % 2)
            store_shared(TT - 1)
            load_rows(4, 0)
            with sp.Fori(0, (SLOT_TILES - 5) // 2) as j:
                for n in range(5, 7):
                    load_rows(j * 2 + n, n % 2)
            sp.wait_ge(sum_st, 16 * SLOT_TILES)
            sp.dma_start(out_d, sum_d[0:T, :]).then_inc(out_st, 16)
            sp.wait_ge(out_st, 16)

        def inverse_deviation(pool, chain, n):
            pool.wait_ge(aggr_ok, n + 1)
            sl = slice(TPG * (n % G), TPG * (n % G) + TPG)
            chain(pool.tensor_scalar(veps[:, sl], mv[:, sl, 1], EPS, 1.0, ALU.add, ALU.mult))
            pool.tensor_tensor(rstd[:, sl], veps[:, sl], neghalf[:, :], ALU.pow).then_inc(rstd_ok, 1)

        def scan_inputs(pool, g):
            with pool.Fori(0, Q // 2) as jj:
                for r in range(2):
                    pool.wait_ge(bc_ld[r], 32 * (Q // 2) * g + 32 + jj * 32)
                    for i in range(IC):
                        n = r * IC + i
                        pool.wait_ge(state_free, STEPS * g + n + 1 + jj * (2 * IC))
                        pool.tensor_tensor(
                            state(n % 3).rearrange("p (n t) -> p n t", n=NQ),
                            u[:, g, i, :].unsqueeze(1).to_broadcast([128, NQ, GT]),
                            bc[:, r, 0, :, :], ALU.mult).then_inc(dbu_ok, 1)

        @block.gpsimd
        def _(pool):
            link = [0]

            def chain(ins):
                link[0] += 1
                ins.then_inc(pool_c, 1)
                pool.wait_ge(pool_c, link[0])

            chain(pool.memset(ident[:, :], 0.0))
            pool.affine_select(out=ident[:, :], in_=ident[:, :], compare_op=ALU.not_equal, fill=1.0, base=0,
                               pattern=[[-1, 128]], channel_multiplier=1).then_inc(ident_ok, 1)
            pool.memset(neghalf[:, :], -0.5).then_inc(ident_ok, 1)
            chain(pool.memset(before[:, :], 1.0))
            pool.affine_select(out=before[:, :], in_=before[:, :], compare_op=ALU.is_gt, fill=0.0, base=0,
                               pattern=[[1, 128]], channel_multiplier=-1).then_inc(consts_ok, 1)
            pool.memset(ones[:, :], 1.0).then_inc(consts_ok, 1)
            pool.iota(iota_i[:, :], pattern=[[1, SLOT_TILES]], base=0, channel_multiplier=0).then_inc(consts_ok, 1)
            chain(pool.iota(token_i[:, :], pattern=[[128, TT + 1]], base=0, channel_multiplier=1))
            pool.tensor_copy(xn[:, :, TOKEN], token_i[:, 0:TT]).then_inc(ids_ok, 1)
            chain(pool.memset(zeros[:, :, :], 0.0))
            pool.tensor_copy(zeros[:, :, TOKEN], token_i[:, TT:TT + 1].to_broadcast([128, 4])).then_inc(zero_ok, 1)
            pool.wait_ge(ident_ok, 2)
            for g in range(G):
                inverse_deviation(pool, chain, g)
            pool.wait_ge(zero_st, 16 * -(-SLOT_TILES // 4))
            pool.wait_ge(spare_st, 16)
            pool.sem_inc(state_free, 3)
            for g in range(G):
                for i in range(IC):
                    pool.wait_ge(dt_ok, IC * g + i + 1)
                    pool.tensor_tensor(u[:, g, i, :], dt[:, g, i, :], h[:, g, i, :], ALU.mult).then_inc(u_ok, 1)
                pool.wait_ge(u_ok, IC * (g + 1))
                scan_inputs(pool, g)
            for v in range(IN_U):
                low_part(pool, v)
            pool.wait_ge(low_ok, IN_U)
            for g in range(G):
                inverse_deviation(pool, chain, G + g)
            for v in range(IN_U, BEFORE_SCATTER):
                low_part(pool, v)
            pool.wait_ge(low_ok, BEFORE_SCATTER)
            pool.wait_ge(pos_ok, 1)
            for t in range(TT):
                for k in range(2):
                    pool.indirect_dma_start(
                        out=rows_d, out_offset=bass.IndirectOffsetOnAxis(ap=pos_i[:, k, t:t + 1], axis=0),
                        in_=xn[:, t, :], in_offset=None).then_inc(scat_st, 16)

            def add_result(n, s, r):
                pool.tensor_copy(token_r[:, r:r + 1], token[:, n]).then_inc(token_ok, 1)
                pool.wait_ge(ysb_ok, s + 1)
                wait(pool, sum_st, s * 16 + 16 * -TT)
                pool.wait_ge(token_ok, s + (1 - TT))
                pool.sem_inc(add_start, 1)
                pool.indirect_dma_start(
                    out=sum_d, out_offset=bass.IndirectOffsetOnAxis(ap=token_r[:, r:r + 1], axis=0),
                    in_=ysb[:, r, :], in_offset=None, compute_op=ALU.add).then_inc(sum_st, 16)

            pool.wait_ge(slots_ok, 1)
            for r in range(2):
                pool.wait_ge(y_st[r], 16 * TT // 2)
            add_result(slice(0, 1), TT, 0)
            with pool.Fori(0, SLOT_TILES // 2) as j:
                for n in range(1, 3):
                    add_result(bass.ds(j * 2 + n, 1), j * 2 + (n + TT), n % 2)

        def transposed_to_sbuf(act, n):
            g = n % G
            act.wait_ge(xn_tr, n + 1)
            bank, end = (2, DB) if n < G else (4, 128)
            act.activation(xnT[:, 0, g * GT:(g + 1) * GT], ps[:, bank, :], ACT.Copy).then_inc(xnT_ok, 1)
            act.activation(xnT[0:end, 1, g * GT:(g + 1) * GT], ps[0:end, bank + 1, :], ACT.Copy).then_inc(xnT_ok, 1)
            if n >= G:
                act.wait_ge(xnT_ok, 2 * (n + 1))

        @block.scalar
        def _(act):
            link = [0]

            def chain(ins):
                link[0] += 1
                ins.then_inc(act_c, 1)
                act.wait_ge(act_c, link[0])

            act.dma_start(projT[:, :, :], projT_d.rearrange("(k p) d -> p k d", p=128)).then_inc(ld_proj, 16)
            act.dma_start(projb[:, :], projb_d.partition_broadcast(128)).then_inc(ld_proj, 16)
            for half in range(2):
                act.dma_start(posb[half * S:(half + 1) * S, :], pos_d).then_inc(ld_proj, 16)
            act.dma_start(inTa[:, :], inT_d[0:DA, :]).then_inc(ld_par, 16)
            act.dma_start(inTb[:, :], inT_d[DA:D, :]).then_inc(ld_par, 16)
            act.dma_start(par[:, :, :], par_d.rearrange("(i p) n -> p i n", p=128)).then_inc(ld_par, 16)
            act.dma_start(xpT[:, :, :], xpT_d.rearrange("(i p) n -> p i n", p=128)).then_inc(ld_mid, 16)
            act.dma_start(dtT[:, :], dtT_d).then_inc(ld_mid, 16)
            act.dma_start(outT[:, :, :], outT_d.rearrange("(i p) n -> p i n", p=128)).then_inc(ld_mid, 16)
            act.dma_start(gateTa[:, :], gateT_d[0:DA, :]).then_inc(ld_mid, 16)
            act.dma_start(gateTb[:, :], gateT_d[DA:D, :]).then_inc(ld_mid, 16)
            act.wait_ge(zero_ok, 1)
            for z in range(0, SLOT_TILES, 4):
                end = min(z + 4, SLOT_TILES)
                act.dma_start(rows_v[z:end].rearrange("s p d -> p s d"), zeros[:, 0:end - z, :]).then_inc(zero_st, 16)
            act.dma_start(sum_v[TT], zeros[:, 0, 0:D]).then_inc(spare_st, 16)
            def conv_silu(g):
                act.wait_ge(conv_ok, g + 1)
                act.activation(h[:, g, :, :], u[:, g, :, :], ACT.Silu).then_inc(h_ok, 1)

            act.wait_ge(pads_ok, 1)
            for g in range(G):
                transposed_to_sbuf(act, g)
                for m in range(2 * IC):
                    n = 2 * IC * g + m
                    act.wait_ge(in_mm, n + 1)
                    if m < IC:
                        act.activation(hp[:, g, m, :, K - 1:],
                                       ps[:, 4 + n % 4, :].rearrange("p (b s) -> p b s", b=GB),
                                       ACT.Copy).then_inc(hidden_ok, 1)
                    else:
                        act.activation(sg[:, g, m - IC, :], ps[:, 4 + n % 4, :], ACT.Silu).then_inc(hidden_ok, 1)
                    if g == 1 and m == IC - 1:
                        conv_silu(0)
            conv_silu(1)
            act.wait_ge(ld_par, 48)
            act.wait_ge(h_ok, G)
            for g in range(G):
                for i in range(IC):
                    act.wait_ge(dt_mm, IC * g + i + 1)
                    act.activation(dt[:, g, i, :], ps[:, 1 + i, :], ACT.Identity,
                                   bias=par[:, i, P_DTB:P_DTB + 1]).then_inc(dt_lin, 1)
                act.wait_ge(dt_lin, IC * (g + 1))
                chain(act.activation(u[:, g, :, :], dt[:, g, :, :], ACT.Abs))
                chain(act.activation(u[:, g, :, :], u[:, g, :, :], ACT.Exp, scale=-1.0))
            for g in range(G):
                for i in range(IC):
                    act.activation(u[:, g, i, :], u[:, g, i, :], ACT.Ln, bias=1.0).then_inc(lnp_ok, 1)
            act.activation(negA[:, :, :], par[:, :, P_A:P_A + N], ACT.Exp).then_inc(expA_ok, 1)
            act.wait_ge(negA_ok, 1)
            for g in range(G):
                act.wait_ge(dt_ok, IC * (g + 1))
                with act.Fori(0, Q // 2) as jj:
                    for n in range(2 * IC):
                        r, i = n // IC, n % IC
                        act.wait_ge(decay_free, STEPS * g + n + 1 + jj * (2 * IC))
                        for q in range(NQ):
                            last = act.activation(
                                decay(n % 2)[:, q, :, 1:],
                                dt[:, g, i, :].rearrange("p (b s) -> p b s", b=GB)[:, :, 1:], ACT.Exp,
                                scale=negA[:, i, :].rearrange("p (j r q) -> p j r q", r=2, q=NQ)[:, jj, r, q:q + 1])
                        last.then_inc(decay_ok, 1)
            act.wait_ge(u_ok, IC * G)
            act.wait_ge(decay_ok, G * STEPS)
            act.wait_ge(state_free, STEPS + 3 + 1)
            for v in range(IN_H_DT):
                high_part(act, v)
            act.wait_ge(state_free, G * STEPS + 3)
            for v in range(IN_H_DT, IN_U):
                high_part(act, v)
            transposed_to_sbuf(act, G)

            def x_high(s, r):
                wait(act, up_c, s - 1)
                if isinstance(s, int) and s < TT:
                    source = xnT[:, :, 128 * s:128 * (s + 1)]
                else:
                    act.wait_ge(xs_tr, s + (1 - TT))
                    source = ps[:, 4, 0:256].rearrange("p (k n) -> p k n", k=2)
                act.activation(xs_high[:, r, :, :], source, ACT.Copy).then_inc(x_high_ok, 1)

            def silu(s, r):
                act.wait_ge(up_a, s + 1)
                wait(act, hm_ok, s - 1)
                act.activation(sa[:, r, :], ps[:, r, :], ACT.Silu).then_inc(sa_ok, 1)

            def h_copy(s, r):
                act.wait_ge(hm_tr, s + 1)
                act.activation(hT[:, r, :, :], ps[:, 5, :].rearrange("p (c n) -> p c n", c=HC),
                               ACT.Copy).then_inc(hT_ok, 1)

            def between(s):
                if s == -1:
                    for v in range(IN_U, BEFORE_SCATTER):
                        high_part(act, v)
                    transposed_to_sbuf(act, G + 1)
                if s == 0:
                    act.wait_ge(lmax_ok, 1)
                    act.activation(sc[:, :, :], lg[:, :, :], ACT.Exp).then_inc(lexp_ok, 1)
                for v in late_halves(s):
                    high_part(act, v)

            stage_loop(act, [(1, silu), (2, x_high), (0, h_copy)], between)

        @block.vector
        def _(dve):
            link = [0]

            def chain(ins):
                link[0] += 1
                ins.then_inc(dve_c, 1)
                dve.wait_ge(dve_c, link[0])

            def layer_norm(n):
                tiles = range(TPG * (n % G), TPG * (n % G) + TPG)
                for t in tiles:
                    last = dve.bn_stats(stats[:, t, :], h0[:, t, :])
                chain(last)
                for t in tiles:
                    last = dve.bn_aggr(mv[:, t, :], stats[:, t, :])
                last.then_inc(aggr_ok, 1)

            def normed(n):
                dve.wait_ge(rstd_ok, n + 1)
                for t in range(TPG * (n % G), TPG * (n % G) + TPG):
                    if n >= G:
                        dve.tensor_scalar(xn[:, t, D:2 * DA], h0[:, t, DA:], mv[:, t, 0:1], rstd[:, t:t + 1],
                                          ALU.subtract, ALU.mult)
                    dve.tensor_scalar(xn[:, t, 0:D], h0[:, t, :], mv[:, t, 0:1], rstd[:, t:t + 1],
                                      ALU.subtract, ALU.mult).then_inc(xn_ok, 1)

            dve.memset(hp[:, :, :, :, 0:K - 1].rearrange("p g i b s -> p (g i b) s"), 0.0).then_inc(pads_ok, 1)
            dve.wait_ge(ld_proj, 64)
            chain(dve.tensor_tensor(posb[:, :], posb[:, :], projb[:, :], ALU.add))
            for g in range(G):
                for t in range(TPG * g, TPG * (g + 1)):
                    dve.wait_ge(patch_mm, t + 1)
                    dve.tensor_tensor(h0[:, t, :], ps[:, t % 2, 0:D], posb[:, :], ALU.add).then_inc(h0_ok, 1)
                if g:
                    normed(0)
                dve.wait_ge(h0_ok, TPG * (g + 1))
                layer_norm(g)
            normed(1)
            dve.wait_ge(consts_ok, 3)
            chain(dve.tensor_copy(iota[:, :], iota_i[:, :]))
            dve.tensor_scalar(steps[:, :], iota[:, 0:TT], 128.0, None, ALU.mult)
            dve.wait_ge(ld_par, 48)
            def scan_coefficients(g):
                dve.wait_ge(xp_mm, g + 1)
                dve.tensor_copy(ssm[:, g, :], ps[0:R + 2 * N, 0, :]).then_inc(ssm_ok, 1)

            for g in range(G):
                for i in range(IC):
                    dve.wait_ge(hidden_ok, 2 * IC * g + i + 1)
                    out = u[:, g, i, :].rearrange("p (b s) -> p b s", b=GB)
                    chain(dve.tensor_scalar(out, hp[:, g, i, :, 0:S], par[:, i, P_CW:P_CW + 1],
                                            par[:, i, P_CB:P_CB + 1], ALU.mult, ALU.add))
                    for k in range(1, K):
                        ins = dve.scalar_tensor_tensor(out, hp[:, g, i, :, k:k + S], par[:, i, P_CW + k:P_CW + k + 1],
                                                       out, ALU.mult, ALU.add)
                        if i == IC - 1 and k == K - 1:
                            ins.then_inc(conv_ok, 1)
                        else:
                            chain(ins)
                if g == 0:
                    dve.wait_ge(ident_ok, 2)
            scan_coefficients(0)
            dve.wait_ge(conv_ok, G)
            for r in range(2):
                dve.memset(decay(r)[:, :, :, 0:1].rearrange("p n b s -> p (n b) s"), 0.0).then_inc(decay_free, 1)
            for i in range(IC):
                dve.tensor_scalar(diagD[:, i, :], ident[:, :], par[:, i, P_D:P_D + 1], None, ALU.mult).then_inc(diag_ok, 1)
            scan_coefficients(1)
            for g in range(G):
                for i in range(IC):
                    dve.wait_ge(lnp_ok, IC * g + i + 1)
                    chain(dve.scalar_tensor_tensor(dt[:, g, i, :], dt[:, g, i, :], 0.0, u[:, g, i, :],
                                                   ALU.max, ALU.add))
                    end = dt[:, g, i, S - 1::S]
                    dve.tensor_scalar(end, end, par[:, i, P_ALPHA:P_ALPHA + 1], None, ALU.mult).then_inc(dt_ok, 1)
            dve.wait_ge(expA_ok, 1)
            dve.tensor_scalar(negA[:, :, :], negA[:, :, :], -1.0, None, ALU.mult).then_inc(negA_ok, 1)
            for g in range(G):
                with dve.Fori(0, Q // 2) as jj:
                    for n in range(2 * IC):
                        r, i = n // IC, n % IC
                        s = STEPS * g + n
                        dve.wait_ge(decay_ok, s + 1 + jj * (2 * IC))
                        dve.wait_ge(dbu_ok, s + 1 + jj * (2 * IC))
                        dve.tensor_tensor_scan(state(n % 3), decays[:, n % 2, :], state(n % 3), 0.0,
                                               ALU.mult, ALU.add).then_inc(decay_free, 1)
                        dve.wait_ge(decay_free, s + 3 + jj * (2 * IC))
                        dve.tensor_tensor(state(n % 3), state(n % 3),
                                          bc[:, r, 1, :, :].rearrange("p n t -> p (n t)"),
                                          ALU.mult).then_inc(cs_ok, 1)
            dve.wait_ge(hidden_ok, 2 * IC * G)
            for g in range(G):
                dve.wait_ge(state_free, STEPS * (g + 1) + 3)
                for i in range(IC):
                    dve.tensor_tensor(sg[:, g, i, :], ps[:, YBANK[g] + i, :], sg[:, g, i, :], ALU.mult).then_inc(yevac, 1)
                dve.wait_ge(yevac, IC * (g + 1))
                for i in range(IC):
                    end = sg[:, g, i, S - 1::S]
                    dve.tensor_scalar(end, end, par[:, i, P_FG:P_FG + 1], None, ALU.mult).then_inc(y_ok, 1)
            dve.wait_ge(xn_tr, G)
            for g in range(G):
                for t in range(TPG * g, TPG * (g + 1)):
                    dve.wait_ge(op_mm, t + 1)
                    dve.tensor_tensor(h0[:, t, :], ps[:, OBANK[t % 2], 0:D], h0[:, t, :], ALU.add).then_inc(h1_ok, 1)
                if g:
                    normed(G)
                dve.wait_ge(h1_ok, TPG * (g + 1))
                layer_norm(G + g)

            def over_e(ap):
                return ap.unsqueeze(2).to_broadcast([128, TT, E])

            def second_rows():
                normed(G + 1)

            def shifted_logits():
                dve.wait_ge(lg_mm, G)
                chain(dve.tensor_copy(lg[:, :, :], ps[:, 7, 0:TT * E].rearrange("p (t e) -> p t e", t=TT)))
                chain(dve.tensor_reduce(red[:, 0, :], lg[:, :, :], AX.X, ALU.max))
                dve.tensor_tensor(lg[:, :, :], lg[:, :, :], over_e(red[:, 0, :]), ALU.subtract).then_inc(lmax_ok, 1)

            def top_two():
                dve.wait_ge(lexp_ok, 1)
                chain(dve.tensor_reduce(red[:, 1, :], sc[:, :, :], AX.X, ALU.add))
                chain(dve.reciprocal(red[:, 1, :], red[:, 1, :]))
                chain(dve.tensor_tensor(sc[:, :, :], sc[:, :, :], over_e(red[:, 1, :]), ALU.mult))
                for t in range(TT):
                    last = dve.max(m8[:, t, :], sc[:, t, :])
                chain(last)
                for t in range(TT):
                    last = dve.max_index(ix[:, t, :], m8[:, t, :], sc[:, t, :])
                chain(last)

            def one_hots():
                for k in range(2):
                    last = dve.tensor_copy(ixf[:, k, :], ix[:, :, k])
                chain(last)
                for k in range(2):
                    last = dve.tensor_tensor(hot[:, k, :, :], iota[:, 0:E].unsqueeze(1).to_broadcast([128, TT, E]),
                                             over_e(ixf[:, k, :]), ALU.is_equal)
                chain(last)
                dve.memset(mcum[:, 0, :], 0.0)
                chain(dve.tensor_tensor(msum[:, :, :], hot[:, 0, :, :], hot[:, 1, :, :], ALU.add))
                for t in range(TT):
                    ins = dve.tensor_tensor(mcum[:, t + 1, :], mcum[:, t, :], msum[:, t, :], ALU.add)
                    if t < TT - 1:
                        chain(ins)
                    else:
                        ins.then_inc(mcum_ok, 1)

            def token_weights():
                chain(dve.tensor_tensor(red[:, 2, :], m8[:, :, 0], m8[:, :, 1], ALU.add))
                chain(dve.tensor_scalar(red[:, 2, :], red[:, 2, :], 1e-20, None, ALU.add))
                chain(dve.reciprocal(red[:, 2, :], red[:, 2, :]))
                dve.wait_ge(ids_ok, 1)
                dve.tensor_copy(xn[:, :, FIRST_EXPERT], ixf[:, 0, :])
                for k in range(2):
                    last = dve.tensor_tensor(xn[:, :, WEIGHT + k], m8[:, :, k], red[:, 2, :], ALU.mult)
                chain(last)

            def tile_counts():
                dve.wait_ge(rank_mm, 1)
                dve.tensor_copy(rank[:, :, :], ps[:, 4, 0:TT * E].rearrange("p (t e) -> p t e", t=TT))
                chain(dve.tensor_copy(cnt[:, :], ps[:, 4, TT * E:(TT + 1) * E]))
                gt_v = gt[:, :].rearrange("p (e k) -> p e k", k=TT)
                chain(dve.tensor_tensor(gt_v, cnt[:, :].unsqueeze(2).to_broadcast([128, E, TT]),
                                        steps[:, :].unsqueeze(1).to_broadcast([128, E, TT]), ALU.is_gt))
                chain(dve.tensor_reduce(ntile[:, :], gt_v, AX.X, ALU.add))
                chain(dve.tensor_tensor_scan(tend[:, :], ones[:, 0:E], ntile[:, :], 0.0, ALU.mult, ALU.add))
                chain(dve.tensor_tensor(base[:, :], tend[:, :], ntile[:, :], ALU.subtract))

            def slots():
                chain(dve.tensor_scalar(base[:, :], base[:, :], 128.0, None, ALU.mult))
                chain(dve.tensor_tensor(rank[:, :, :], rank[:, :, :],
                                        base[:, :].unsqueeze(1).to_broadcast([128, TT, E]), ALU.add))
                for k in range(2):
                    last = dve.tensor_tensor(hot[:, k, :, :], hot[:, k, :, :], rank[:, :, :], ALU.mult)
                chain(last)
                chain(dve.tensor_reduce(posf[:, :, :], hot[:, :, :, :], AX.X, ALU.add))
                dve.tensor_copy(pos_i[:, :, :], posf[:, :, :]).then_inc(pos_ok, 1)

            def tile_experts():
                chain(dve.tensor_tensor(tcmp[:, :, :], iota[:, :].unsqueeze(2).to_broadcast([128, SLOT_TILES, E]),
                                        tend[:, :].unsqueeze(1).to_broadcast([128, SLOT_TILES, E]), ALU.is_ge))
                chain(dve.tensor_reduce(tef[:, :], tcmp[:, :, :], AX.X, ALU.add))
                chain(dve.tensor_scalar(tef[:, :], tef[:, :], float(E - 1), None, ALU.min))
                dve.tensor_copy(te[:, :], tef[:, :]).then_inc(te_ok, 1)

            def slot_weights():
                dve.wait_ge(info_ld, 16)
                dve.tensor_copy(token[:, :], info[:, :, TOKEN - 2 * DA])
                for k, same in enumerate((ALU.is_equal, ALU.not_equal)):
                    last = dve.tensor_tensor(chosen[:, k, :], info[:, :, FIRST_EXPERT - 2 * DA], tef[:, :], same)
                chain(last)
                for k in range(2):
                    last = dve.tensor_tensor(chosen[:, k, :], chosen[:, k, :], info[:, :, WEIGHT + k - 2 * DA], ALU.mult)
                chain(last)
                dve.tensor_tensor(weight[:, :], chosen[:, 0, :], chosen[:, 1, :], ALU.add).then_inc(slots_ok, 1)
                dve.wait_ge(slots_ok, 1)
                for r in range(2):
                    dve.wait_ge(y_st[r], 16 * TT // 2)

            def x_low(s, r):
                dve.wait_ge(x_high_ok, s + 1)
                if isinstance(s, int) and s < TT:
                    source = xnT[:, :, 128 * s:128 * (s + 1)]
                else:
                    source = ps[:, 4, 0:256].rearrange("p (k n) -> p k n", k=2)
                dve.tensor_tensor(xs_low[:, r, :, :], source, xs_high[:, r, :, :].bitcast(F32),
                                  ALU.subtract).then_inc(x_low_ok, 1)

            def gated(s, r):
                dve.wait_ge(up_c, s + 1)
                dve.wait_ge(sa_ok, s + 1)
                dve.tensor_tensor(hm[:, r, :], ps[:, 2 + r, :], sa[:, r, :], ALU.mult).then_inc(hm_ok, 1)

            def result(s, r):
                dve.wait_ge(down_mm, s + 1)
                if isinstance(s, int) and s < TT:
                    wait(dve, y_st[r], 16 * (s // 2))
                    dve.tensor_tensor(ysb[:, r, :], ps[:, 6 + r, 0:D], h0[:, s, :], ALU.add).then_inc(ysb_ok, 1)
                    return
                if not isinstance(s, int) or s >= TT + 2:
                    dve.wait_ge(sum_st, s * 16 + -16 * (TT + 1))
                n = slice(s - TT, s - TT + 1) if isinstance(s, int) else bass.ds(s + -TT, 1)
                dve.tensor_tensor(ysb[:, r, :], ps[:, 6 + r, 0:D], weight[:, n].to_broadcast([128, D]),
                                  ALU.mult).then_inc(ysb_ok, 1)

            def between(s):
                for stage in {-1: (second_rows,), 0: (shifted_logits, top_two, one_hots),
                              1: (token_weights, tile_counts, slots), 2: (tile_experts,), TT + 1: (slot_weights,)}.get(s, ()):
                    stage()
                for v in late_halves(s):
                    low_part(dve, v)

            stage_loop(dve, [(1, gated), (2, x_low), (-1, result)], between)

        @block.tensor
        def _(pe):
            def transposes(n):
                g = n % G
                pe.wait_ge(xn_ok, TPG * (n + 1))
                if n:
                    pe.wait_ge(xnT_ok, 2 * n)
                bank, end = (2, DB) if n < G else (4, 128)
                for q in range(TPG):
                    t = TPG * g + q
                    pe.transpose(ps[:, bank, 128 * q:128 * (q + 1)], xn[:, t, 0:DA], ident[:, :])
                    last = pe.transpose(ps[0:end, bank + 1, 128 * q:128 * (q + 1)], xn[:, t, DA:DA + end], ident[:, :])
                last.then_inc(xn_tr, 1)

            pe.wait_ge(ld_proj, 64)
            for t in range(TT):
                if t % TPG == 0:
                    pe.wait_ge(ld_x[t // TPG], 16)
                if t >= 2:
                    pe.wait_ge(h0_ok, t - 1)
                for k in range(PK):
                    last = pe.matmul(ps[:, t % 2, 0:D], xT[:, k, 128 * t:128 * (t + 1)], projT[:, k, :],
                                     start=(k == 0), stop=(k == PK - 1))
                last.then_inc(patch_mm, 1)
            pe.wait_ge(ident_ok, 2)
            for g in range(G):
                transposes(g)
                pe.wait_ge(xnT_ok, 2 * (g + 1))
                if g == 0:
                    pe.wait_ge(ld_par, 48)
                for m in range(2 * IC):
                    n = 2 * IC * g + m
                    if n >= 4:
                        pe.wait_ge(hidden_ok, n - 3)
                    pe.matmul(ps[:, 4 + n % 4, :], inTa[:, 128 * m:128 * (m + 1)], xnT[:, 0, GT * g:GT * (g + 1)],
                              start=True, stop=False)
                    pe.matmul(ps[:, 4 + n % 4, :], inTb[:, 128 * m:128 * (m + 1)], xnT[0:DB, 1, GT * g:GT * (g + 1)],
                              start=False, stop=True).then_inc(in_mm, 1)
            pe.wait_ge(ld_mid, 80)
            pe.wait_ge(h0_ok, TT)
            pe.wait_ge(xnT_ok, 2 * G)
            for g in range(G):
                pe.wait_ge(h_ok, g + 1)
                for i in range(IC):
                    last = pe.matmul(ps[0:R + 2 * N, 0, :], xpT[:, i, :], h[:, g, i, :], start=(i == 0), stop=(i == IC - 1))
                last.then_inc(xp_mm, 1)
                pe.wait_ge(ssm_ok, g + 1)
                if g:
                    pe.wait_ge(dt_lin, IC * g)
                for i in range(IC):
                    pe.matmul(ps[:, 1 + i, :], dtT[:, 128 * i:128 * (i + 1)], ssm[0:R, g, :],
                              start=True, stop=True).then_inc(dt_mm, 1)
            pe.wait_ge(diag_ok, IC)
            for g in range(G):
                pe.wait_ge(*((hidden_ok, 2 * IC * G), (dt_lin, IC * G))[g])
                for i in range(IC):
                    pe.matmul(ps[:, YBANK[g] + i, :], diagD[:, i, :], h[:, g, i, :], start=True, stop=True)
                with pe.Fori(0, Q // 2) as jj:
                    for n in range(2 * IC):
                        pe.wait_ge(cs_ok, STEPS * g + n + 1 + jj * (2 * IC))
                        for q in range(NQ):
                            last = pe.matmul(ps[:, YBANK[g] + n % IC, :], ident[:, :], state(n % 3)[:, q * GT:(q + 1) * GT],
                                             start=False, stop=True, skip_group_check=True)
                        last.then_inc(state_free, 1)
            for t in range(TT):
                g, q = t // TPG, t % TPG
                if q == 0:
                    pe.wait_ge(y_ok, IC * (g + 1))
                if t >= 2:
                    pe.wait_ge(h1_ok, t - 1)
                for i in range(IC):
                    last = pe.matmul(ps[:, OBANK[t % 2], 0:D], sg[:, g, i, 128 * q:128 * (q + 1)], outT[:, i, :],
                                     start=(i == 0), stop=(i == IC - 1))
                last.then_inc(op_mm, 1)
            pe.wait_ge(h1_ok, TT)

            def logits(g):
                pe.wait_ge(xnT_ok, 2 * (G + g + 1))
                for t in range(TPG * g, TPG * (g + 1)):
                    o = ps[:, 7, t * E:(t + 1) * E]
                    pe.matmul(o, xnT[:, 0, 128 * t:128 * (t + 1)], gateTa[:, :], start=True, stop=False)
                    last = pe.matmul(o, xnT[0:DB, 1, 128 * t:128 * (t + 1)], gateTb[:, :], start=False, stop=True)
                last.then_inc(lg_mm, 1)

            def x_transposes(s, r):
                if isinstance(s, int) and s < TT:
                    return
                pe.wait_ge(xs_ld[r], s * 8 + (16 - 8 * r - 8 * TT))
                pe.wait_ge(x_low_ok, s)
                pe.transpose(ps[:, 4, 0:128], xs[:, r, 0:DA], ident[:, :])
                pe.transpose(ps[:, 4, 128:256], xs[:, r, DA:], ident[:, :]).then_inc(xs_tr, 1)

            def expert(weights, s):
                if isinstance(s, int) and s < TT:
                    return weights[:, 0]
                n = slice(s - TT, s - TT + 1) if isinstance(s, int) else bass.ds(s + -TT, 1)
                return weights[:, 1:E + 1][:, pe.value_load(te[0:1, n], min_val=0, max_val=E - 1)]

            def up(s, r):
                we = expert(w13, s)
                pe.wait_ge(x_low_ok, s + 1)
                wait(pe, hm_ok, s - 1)
                high, low = xs_high[:, r, :, :], xs_low[:, r, :, :]
                for c, done in ((0, up_a), (1, up_c)):
                    o = ps[:, 2 * c + r, :]
                    wh, wl, ends = (we[:, k, c * HID:(c + 1) * HID] for k in range(3))
                    pe.matmul(o, high[:, 0, :], wh, start=True, stop=False)
                    pe.matmul(o, high[:, 0, :], wl, start=False, stop=False)
                    pe.matmul(o, low[:, 0, :], wh, start=False, stop=False)
                    pe.matmul(o, low[:, 0, :], wl, start=False, stop=False)
                    pe.matmul(o, high[:, 1, :], ends, start=False, stop=False)
                    pe.matmul(o, low[:, 1, :], ends, start=False, stop=True).then_inc(done, 1)

            def h_transposes(s, r):
                pe.wait_ge(hm_ok, s + 1)
                wait(pe, hT_ok, s)
                for c in range(HC):
                    last = pe.transpose(ps[:, 5, 128 * c:128 * (c + 1)], hm[:, r, 128 * c:128 * (c + 1)], ident[:, :])
                last.then_inc(hm_tr, 1)

            def down(s, r):
                we = expert(w2, s)
                pe.wait_ge(hT_ok, s + 1)
                wait(pe, ysb_ok, s - 1)
                for c in range(HC):
                    last = pe.matmul(ps[:, 6 + r, 0:D], hT[:, r, c, :], we[:, c * D:(c + 1) * D],
                                     start=(c == 0), stop=(c == HC - 1))
                last.then_inc(down_mm, 1)

            def between(s):
                if s == -2:
                    transposes(G)
                    logits(0)
                    transposes(G + 1)
                    pe.wait_ge(ld_w2, 16 * (E + 1))
                    pe.wait_ge(low_ok, 2)
                if s == 0:
                    logits(1)
                if s == 1:
                    pe.wait_ge(mcum_ok, 1)
                    pe.wait_ge(consts_ok, 3)
                    o = ps[:, 4, 0:(TT + 1) * E]
                    pe.matmul(o, ones[:, :], mcum[:, :, :].rearrange("p t e -> p (t e)"), start=True, stop=True)
                    pe.matmul(o[:, 0:TT * E], before[:, :], msum[:, :, :].rearrange("p t e -> p (t e)"),
                              start=False, stop=True, skip_group_check=True).then_inc(rank_mm, 1)
                if s == TT - 1:
                    pe.wait_ge(te_ok, 1)
                    pe.wait_ge(low_ok, len(HALVES))

            stage_loop(pe, [(1, up), (2, x_transposes), (0, h_transposes), (-1, down)], between)


_ARRAYS = ("xT", "projT", "projb", "pos", "inT", "params", "xpT", "dtT", "outT", "gateT", "w13T", "w2T")


def kernel(x, L0_tok_proj_w, L0_tok_proj_b, L0_tok_pos_emb, L0_attn_in_proj_w, L0_attn_conv_w, L0_attn_conv_b,
           L0_attn_x_proj_w, L0_attn_dt_proj_w, L0_attn_dt_proj_b, L0_attn_A_log, L0_attn_D, L0_attn_out_proj_w,
           L0_attn_alpha, L0_attn_feature_gating, L0_ffn_gate_w, L0_ffn_w1, L0_ffn_w2, L0_ffn_w3,
           L0_ffn_ws1, L0_ffn_ws2, L0_ffn_ws3):
    import concourse.bacc as bacc
    from concourse.bass_utils import run_bass_kernel_spmd

    a = np.asarray
    col = lambda v: a(v).reshape(I, 1)
    side = IMG // PATCH
    w1 = np.concatenate([a(L0_ffn_ws1)[None], a(L0_ffn_w1)]).transpose(0, 2, 1)
    w3 = np.concatenate([a(L0_ffn_ws3)[None], a(L0_ffn_w3)]).transpose(0, 2, 1)
    laid = {
        "xT": (a(x).reshape(B, C_IN, side, PATCH, side, PATCH).transpose(0, 1, 2, 4, 3, 5)
               .reshape(T, PD).T),
        "projT": a(L0_tok_proj_w).T,
        "projb": a(L0_tok_proj_b),
        "pos": a(L0_tok_pos_emb)[0],
        "inT": a(L0_attn_in_proj_w).T,
        "params": np.concatenate([a(L0_attn_conv_w)[:, 0], col(L0_attn_conv_b), col(L0_attn_dt_proj_b),
                                  a(L0_attn_A_log), col(L0_attn_D), col(L0_attn_alpha),
                                  col(L0_attn_feature_gating)], axis=1),
        "xpT": a(L0_attn_x_proj_w).T,
        "dtT": a(L0_attn_dt_proj_w).T,
        "outT": a(L0_attn_out_proj_w).T,
        "gateT": a(L0_ffn_gate_w).T,
        "w13T": np.concatenate([w1, w3], axis=2),
        "w2T": np.concatenate([a(L0_ffn_ws2)[None], a(L0_ffn_w2)]).transpose(0, 2, 1),
    }
    laid = {n: np.ascontiguousarray(v) for n, v in laid.items()}
    nc = bacc.Bacc("TRN2", target_bir_lowering=False, num_devices=1)
    args = [nc.dram_tensor("in_" + n, laid[n].shape, F32, kind="ExternalInput").ap() for n in _ARRAYS]
    out = nc.dram_tensor("out", (T, D), F32, kind="ExternalOutput").ap()
    program(nc, *args, out)
    r = run_bass_kernel_spmd(nc, [{"in_" + n: v for n, v in laid.items()}], core_ids=[0])
    return r.results[0]["out"].reshape(B, S, D)
```

```python
import numpy as np
import concourse.bass as bass
import concourse.mybir as mybir
from concourse.alu_op_type import AluOpType as ALU
from contextlib import ExitStack

F32 = mybir.dt.float32
F32R = mybir.dt.float32r
I32 = mybir.dt.int32
U32 = mybir.dt.uint32
ACT = mybir.ActivationFunctionType
AX = mybir.AxisListType

B, C_IN, IMG, PATCH = 16, 2, 128, 16
S = (IMG // PATCH) ** 2
D = 192
DA, DB = 128, D - 128
PD = C_IN * PATCH * PATCH
PK = PD // 128
T = B * S
TT = T // 128
G = 2
GT = T // G
GB = B // G
TPG = TT // G
I = 384
IC = I // 128
N = 16
R = 48
K = 4
NQ = 4
Q = N // NQ
E = 8
HID = 512
HC = HID // 128
SLOT_TILES = (2 * T + E * 127) // 128
TILES = TT + SLOT_TILES
ROW = 2 * DA + 4
FIRST_EXPERT, WEIGHT, TOKEN = 2 * DA, 2 * DA + 1, 2 * DA + 3
EPS = 1e-5
PARAMS = K + 1 + 1 + N + 1 + 1 + 1
P_CW, P_CB, P_DTB, P_A, P_D, P_ALPHA, P_FG = 0, K, K + 1, K + 2, K + 2 + N, K + 3 + N, K + 4 + N


def program(nc, xT_d, projT_d, projb_d, pos_d, inT_d, par_d, xpT_d, dtT_d, outT_d, gateT_d, w13T_d, w2T_d, out_d):
    ctx = ExitStack()
    with ctx:
        def sb(name, shape, dt=F32):
            return ctx.enter_context(nc.sbuf_tensor(name, shape, dt))

        def sem(name):
            return ctx.enter_context(nc.semaphore(name))

        bc_d = nc.dram_tensor("bc_scratch", [2, G * N, GT], F32).ap()
        rows_d = nc.dram_tensor("rows_scratch", [SLOT_TILES * 128, ROW], F32).ap()

        STAGE = 3
        front_at = -(-nc.sbuf_base // 32) * 32
        sb("front_memory", [128, 3584])
        at = [front_at]

        def place(name, shape, dt=F32):
            size = -(-4 * int(np.prod(shape[1:])) // 32) * 32
            t = nc.alloc_sbuf_tensor_at(name, shape, dt, offset=at[0])
            at[0] += size
            return t

        projT = place("projT", [128, PK, D])
        inTa = place("inTa", [DA, 2 * I])
        inTb = place("inTb", [DB, 2 * I])
        xpT = place("xpT", [128, IC, R + 2 * N])
        dtT = place("dtT", [R, I])
        posb = place("posb", [128, D])
        projb = place("projb", [128, D])
        assert at[0] <= front_at + 4 * 3584
        at[0] = front_at
        raw = place("raw", [128, STAGE, 2 * HID])
        W13 = 3 * 2 * HID
        scan_at = -(-nc.sbuf_base // 32) * 32
        sb("scan_memory", [128, (E + 1) * W13])
        at[0] = scan_at
        h = place("h", [128, G, IC, GT])
        dt = place("dt", [128, G, IC, GT])
        u = place("u", [128, G, IC, GT])
        decays = place("decays", [128, 2, NQ * GT])
        states = place("states", [128, 3, NQ * GT])
        bc = place("bc", [128, 2, 2, NQ, GT])
        assert at[0] <= scan_at + 4 * (E + 1) * W13
        at[0] = scan_at
        w13 = place("w13", [128, E + 1, 3, 2 * HID], F32R)
        par = sb("par", [128, IC, PARAMS])
        negA = sb("negA", [128, IC, N])
        diagD = sb("diagD", [128, IC, 128])
        outT = sb("outT", [128, IC, D])
        gateTa = sb("gateTa", [DA, E])
        gateTb = sb("gateTb", [DB, E])
        w2 = sb("w2", [128, E + 1, HC * D])
        ident = sb("ident", [128, 128])
        ones = sb("ones", [128, 128])
        before = sb("before", [128, 128])
        iota_i = sb("iota_i", [128, SLOT_TILES], I32)
        iota = sb("iota", [128, SLOT_TILES])
        steps = sb("steps", [128, TT])
        neghalf = sb("neghalf", [128, TPG])
        h0 = sb("h0", [128, TT, D])
        xn = sb("xn", [128, TT, ROW])
        stats = sb("stats", [128, TT, 6])
        mv = sb("mv", [128, TT, 2])
        veps = sb("veps", [128, TT])
        rstd = sb("rstd", [128, TT])
        xnT = sb("xnT", [128, 2, T])
        ssm = sb("ssm", [R + 2 * N, G, GT])
        sg_at = -(-nc.sbuf_base // 32) * 32
        sg = sb("sg", [128, G, IC, GT])
        lg = sb("lg", [128, TT, E])
        sc = sb("sc", [128, TT, E])
        red = sb("red", [128, 4, TT])
        m8 = sb("m8", [128, TT, 8])
        ix = sb("ix", [128, TT, 8], U32)
        ixf = sb("ixf", [128, 2, TT])
        hot = sb("hot", [128, 2, TT, E])
        msum = sb("msum", [128, E, TT + 1])
        mcum = sb("mcum", [128, E, TT + 1])
        same_expert = sb("same_expert", [128, E, TT + 1])
        rank = sb("rank", [128, TT, E])
        cnt = sb("cnt", [128, E])
        gt = sb("gt", [128, E * TT])
        ntile = sb("ntile", [128, E])
        tend = sb("tend", [128, E])
        base = sb("base", [128, E])
        posf = sb("posf", [128, 2, TT])
        pos_i = sb("pos_i", [128, 2, TT], I32)
        tcmp = sb("tcmp", [128, SLOT_TILES, E])
        tef = sb("tef", [128, SLOT_TILES])
        te = sb("te", [128, SLOT_TILES], I32)
        token_i = sb("token_i", [128, TT + 1], I32)
        info = sb("info", [128, SLOT_TILES, ROW - 2 * DA])
        chosen = sb("chosen", [128, 2, SLOT_TILES])
        weight = sb("weight", [128, SLOT_TILES])
        token = sb("token", [128, SLOT_TILES], I32)
        token_r = sb("token_r", [128, 2], I32)
        xs = sb("xs", [128, 2, 2 * DA])
        xs_high = sb("xs_high", [128, 2, 2, 128], F32R)
        xs_low = sb("xs_low", [128, 2, 2, 128], F32R)
        ysb = sb("ysb", [128, 2, D])
        at[0] = sg_at
        sa = place("sa", [128, 2, HID])
        hm = place("hm", [128, 2, HID])
        hT = place("hT", [128, 2, HC, 128])
        assert at[0] <= sg_at + 4 * G * IC * GT
        xT = bc[:, :, :, :, :].rearrange("p a b q t -> p (a b q t)")[:, 0:PK * T].rearrange("p (k t) -> p k t", k=PK)
        hp = decays[:, :, :].rearrange("p r n -> p (r n)")[:, 0:G * IC * GB * (S + K - 1)].rearrange(
            "p (g i b s) -> p g i b s", g=G, i=IC, b=GB)
        zeros = states[:, 0, 0:4 * ROW].rearrange("p (s d) -> p s d", s=4)

        ps = ctx.enter_context(nc.psum_tensor("ps", [128, 8, 512], F32))

        def decay(r):
            return decays[:, r, :].rearrange("p (n b s) -> p n b s", n=NQ, b=GB)

        def state(r):
            return states[:, r, :]

        ld_x = [sem(f"ld_x{n}") for n in range(TPG + 1)]
        ld_proj = sem("ld_proj")
        ld_pos = sem("ld_pos")
        ld_par = sem("ld_par")
        ld_mid = sem("ld_mid")
        ld_w2 = sem("ld_w2")
        raw_ld = [sem(f"raw_ld{r}") for r in range(STAGE)]
        high_ok = sem("high_ok")
        low_ok = sem("low_ok")
        ident_ok = sem("ident_ok")
        pool_c = sem("pool_c")
        dve_c = sem("dve_c")
        act_c = sem("act_c")
        consts_ok = sem("consts_ok")
        patch_mm = sem("patch_mm")
        h0_ok = sem("h0_ok")
        aggr_ok = sem("aggr_ok")
        rstd_ok = sem("rstd_ok")
        xn_ok = sem("xn_ok")
        ends_ok = sem("ends_ok")
        xn_tr = sem("xn_tr")
        xnT_ok = sem("xnT_ok")
        in_mm = sem("in_mm")
        pads_ok = sem("pads_ok")
        hidden_ok = sem("hidden_ok")
        conv_ok = sem("conv_ok")
        h_ok = sem("h_ok")
        xp_mm = sem("xp_mm")
        ssm_ok = sem("ssm_ok")
        bc_st = [sem(f"bc_st{g}") for g in range(G)]
        b_ld = [sem(f"b_ld{r}") for r in range(2)]
        c_ld = [sem(f"c_ld{r}") for r in range(2)]
        dt_mm = sem("dt_mm")
        dt_lin = sem("dt_lin")
        lnp_ok = sem("lnp_ok")
        expA_ok = sem("expA_ok")
        negA_ok = sem("negA_ok")
        diag_ok = sem("diag_ok")
        dt_ok = sem("dt_ok")
        u_ok = sem("u_ok")
        decay_free = sem("decay_free")
        state_free = sem("state_free")
        decay_ok = sem("decay_ok")
        dbu_ok = sem("dbu_ok")
        cs_ok = sem("cs_ok")
        yevac = sem("yevac")
        y_ok = sem("y_ok")
        op_mm = sem("op_mm")
        h1_ok = sem("h1_ok")
        zero_ok = sem("zero_ok")
        zero_st = sem("zero_st")
        ids_ok = sem("ids_ok")
        lg_mm = sem("lg_mm")
        lmax_ok = sem("lmax_ok")
        lexp_ok = sem("lexp_ok")
        mcum_ok = sem("mcum_ok")
        rank_mm = sem("rank_mm")
        pos_ok = sem("pos_ok")
        te_ok = sem("te_ok")
        scat_st = sem("scat_st")
        xs_ld = [sem(f"xs_ld{r}") for r in range(2)]
        xs_tr = sem("xs_tr")
        x_high_ok = sem("x_high_ok")
        x_low_ok = sem("x_low_ok")
        up_a = sem("up_a")
        up_c = sem("up_c")
        sa_ok = sem("sa_ok")
        hm_ok = sem("hm_ok")
        hm_tr = sem("hm_tr")
        hT_ok = sem("hT_ok")
        down_mm = sem("down_mm")
        ysb_ok = sem("ysb_ok")
        y_st = [sem(f"y_st{r}") for r in range(2)]
        info_ld = sem("info_ld")
        slots_ok = sem("slots_ok")
        token_ok = sem("token_ok")
        add_start = sem("add_start")
        spare_st = sem("spare_st")
        sum_st = sem("sum_st")

        STEPS = Q * IC
        YBANK = (4, 1)
        OBANK = (0, 7)
        GATES_LATE = 1
        ORDER = [(0, 0), (0, 1), (0, 2), (1, 0), (1, 1), (1, 2), (0, 3), (0, 4), (0, 5), (1, 3), (1, 4), (1, 5)]
        PROJ_BANK = [4, 5, 6, 7, 4, 5, 7, 0, 1, 2, 3, 7]
        rows_v = rows_d.rearrange("(s p) d -> s p d", p=128)
        sum_v = out_d.rearrange("(s p) d -> s p d", p=128)

        HALVES = [(e, half) for e in range(E + 1) for half in range(2)]

        IN_H_DT, IN_U, BEFORE_SCATTER = 4, 6, 8

        def late_halves(s):
            first = BEFORE_SCATTER + 2 * (s - 2)
            return range(max(first, BEFORE_SCATTER), min(first + 2, len(HALVES)))

        def high_part(act, v):
            e, half = HALVES[v]
            act.wait_ge(raw_ld[v % STAGE], raw_count(v))
            act.activation(w13[:, e, 2 * half, :], raw[:, v % STAGE, :], ACT.Copy).then_inc(high_ok, 1)

        def raw_count(v):
            return 16 * sum(1 + HALVES[x][1] for x in range(v % STAGE, v + 1, STAGE))

        def low_part(eng, v):
            e, half = HALVES[v]
            eng.wait_ge(high_ok, v + 1)
            wait(eng, low_ok, v)
            rows = slice(DB * half, 128)
            eng.tensor_tensor(w13[rows, e, 1 + half, :], raw[rows, v % STAGE, :],
                              w13[rows, e, 2 * half, :].bitcast(F32), ALU.subtract).then_inc(low_ok, 1)

        def wait(eng, signal, count):
            if not isinstance(count, int) or count > 0:
                eng.wait_ge(signal, count)

        block = ctx.enter_context(nc.Block())

        LOOP_START = TT + 5
        assert (TILES - 2 - LOOP_START) % 2 == 0

        def stage_loop(eng, parts, between=None):
            def step(s, r, ends):
                for lag, part in parts:
                    if not ends or 0 <= s + lag < TILES:
                        part(s + lag, (r + lag) % 2)

            for s in range(-2, LOOP_START):
                if between:
                    between(s)
                step(s, s % 2, True)
            with eng.Fori(0, (TILES - 2 - LOOP_START) // 2) as j:
                for s in range(LOOP_START, LOOP_START + 2):
                    step(j * 2 + s, s % 2, False)
            for s in range(TILES - 2, TILES + 1):
                step(s, s % 2, True)

        @block.sync
        def _(sp):
            xT_v = xT_d.rearrange("(k p) t -> p k t", p=128)
            for t in range(TPG):
                sp.dma_start(xT[:, :, 128 * t:128 * (t + 1)], xT_v[:, :, 128 * t:128 * (t + 1)]).then_inc(ld_x[t], 16)
            sp.dma_start(xT[:, :, GT:T], xT_v[:, :, GT:T]).then_inc(ld_x[TPG], 16)

            def load_half(v):
                e, half = HALVES[v]
                wait(sp, low_ok, v - STAGE + 1)
                if half == 0:
                    sp.dma_start(raw[:, v % STAGE, :], w13T_d[e, 0:DA, :]).then_inc(raw_ld[v % STAGE], 16)
                else:
                    for rows in (slice(0, DB), slice(DB, 128)):
                        sp.dma_start(raw[rows, v % STAGE, :], w13T_d[e, DA:D, :]).then_inc(raw_ld[v % STAGE], 16)

            def load_quad(z, r):
                for b, (used, loaded) in enumerate(((dbu_ok, b_ld[r]), (cs_ok, c_ld[r]))):
                    wait(sp, used, z * IC - IC)
                    sp.dma_start(bc[:, r, b, :, :],
                                 bc_d[b].rearrange("(z q) t -> z q t", q=NQ)[z].partition_broadcast(128)
                                 ).then_inc(loaded, 16)

            def store_coefficients(g):
                sp.wait_ge(ssm_ok, g + 1)
                for b in range(2):
                    sp.dma_start(bc_d[b, g * N:(g + 1) * N, :],
                                 ssm[R + b * N:R + (b + 1) * N, g, :]).then_inc(bc_st[g], 16)

            store_coefficients(0)
            sp.wait_ge(patch_mm, TT)
            sp.wait_ge(bc_st[0], 32)
            for z in range(Q):
                load_quad(z, z % 2)
            store_coefficients(1)
            sp.wait_ge(bc_st[1], 32)
            with sp.Fori(0, Q // 2) as zz:
                for r in range(2):
                    load_quad(zz * 2 + (r + Q), r)
            sp.wait_ge(dt_lin, IC * G)
            sp.wait_ge(in_mm, 4 * IC)
            for v in range(STAGE):
                load_half(v)
            for e in range(E + 1):
                sp.dma_start(w2[:, e, :].rearrange("p (c d) -> p c d", c=HC),
                             w2T_d[e].rearrange("(c p) d -> p c d", p=128)).then_inc(ld_w2, 16)
            for v in range(STAGE, BEFORE_SCATTER + STAGE):
                load_half(v)

            def load_rows(n, r):
                wait(sp, xs_tr, n - 1)
                sp.dma_start(xs[:, r, :], rows_v[n][:, 0:2 * DA]).then_inc(xs_ld[r], 16)

            def store_shared(n):
                sp.wait_ge(ysb_ok, n + 1)
                sp.dma_start(sum_v[n], ysb[:, n % 2, :]).then_inc(y_st[n % 2], 16)

            EARLY = TT // 2 + 1
            for n in range(EARLY):
                for v in late_halves(n + 1):
                    if v + STAGE < len(HALVES):
                        load_half(v + STAGE)
                store_shared(n)
            sp.wait_ge(scat_st, 16 * 2 * TT)
            for n in range(2):
                load_rows(n, n)
            sp.dma_start(info[:, :, :], rows_v[:, :, 2 * DA:].rearrange("s p d -> p s d")).then_inc(info_ld, 16)
            for n in range(EARLY, TT - 1):
                store_shared(n)
            for n in range(2, 4):
                load_rows(n, n % 2)
            store_shared(TT - 1)
            load_rows(4, 0)
            with sp.Fori(0, (SLOT_TILES - 5) // 2) as j:
                for n in range(5, 7):
                    load_rows(j * 2 + n, n % 2)
            sp.wait_ge(sum_st, 16 * SLOT_TILES)

        def inverse_deviation(pool, chain, n):
            pool.wait_ge(aggr_ok, n + 1)
            sl = slice(TPG * (n % G), TPG * (n % G) + TPG)
            chain(pool.tensor_scalar(veps[:, sl], mv[:, sl, 1], EPS, 1.0, ALU.add, ALU.mult))
            pool.tensor_tensor(rstd[:, sl], veps[:, sl], neghalf[:, :], ALU.pow).then_inc(rstd_ok, 1)

        def scan_input(pool, g, n, jj):
            r, i = n // IC, n % IC
            if i == 0:
                pool.wait_ge(b_ld[r], 16 * (Q // 2) * g + 16 + jj * 16)
            pool.wait_ge(state_free, STEPS * g + n + 1 + jj * (2 * IC))
            pool.tensor_tensor(state(n % 3).rearrange("p (n t) -> p n t", n=NQ),
                               u[:, g, i, :].unsqueeze(1).to_broadcast([128, NQ, GT]),
                               bc[:, r, 0, :, :], ALU.mult).then_inc(dbu_ok, 1)

        @block.gpsimd
        def _(pool):
            link = [0]

            def chain(ins):
                link[0] += 1
                ins.then_inc(pool_c, 1)
                pool.wait_ge(pool_c, link[0])

            chain(pool.memset(ident[:, :], 0.0))
            pool.affine_select(out=ident[:, :], in_=ident[:, :], compare_op=ALU.not_equal, fill=1.0, base=0,
                               pattern=[[-1, 128]], channel_multiplier=1).then_inc(ident_ok, 1)
            pool.memset(neghalf[:, :], -0.5).then_inc(ident_ok, 1)
            chain(pool.memset(before[:, :], 1.0))
            pool.affine_select(out=before[:, :], in_=before[:, :], compare_op=ALU.is_gt, fill=0.0, base=0,
                               pattern=[[1, 128]], channel_multiplier=-1).then_inc(consts_ok, 1)
            pool.memset(ones[:, :], 1.0).then_inc(consts_ok, 1)
            pool.iota(iota_i[:, :], pattern=[[1, SLOT_TILES]], base=0, channel_multiplier=0).then_inc(consts_ok, 1)
            chain(pool.iota(token_i[:, :], pattern=[[128, TT + 1]], base=0, channel_multiplier=1))
            pool.tensor_copy(xn[:, :, TOKEN], token_i[:, 0:TT]).then_inc(ids_ok, 1)
            chain(pool.memset(zeros[:, :, :], 0.0))
            pool.tensor_copy(zeros[:, :, TOKEN], token_i[:, TT:TT + 1].to_broadcast([128, 4])).then_inc(zero_ok, 1)
            pool.wait_ge(ident_ok, 2)
            for g in range(G):
                inverse_deviation(pool, chain, g)
            pool.wait_ge(zero_st, 16 * -(-SLOT_TILES // 4))
            pool.wait_ge(spare_st, 16)
            pool.sem_inc(state_free, 3)
            for s in range(STEPS):
                pool.wait_ge(u_ok, min(s + 1, IC))
                scan_input(pool, 0, s % (2 * IC), s // (2 * IC))
            for i in range(IC):
                pool.wait_ge(dt_ok, IC + i + 1)
                pool.tensor_tensor(u[:, 1, i, :], dt[:, 1, i, :], h[:, 1, i, :], ALU.mult).then_inc(u_ok, 1)
            pool.wait_ge(u_ok, IC * G)
            with pool.Fori(0, Q // 2) as jj:
                for n in range(2 * IC):
                    scan_input(pool, 1, n, jj)
            for v in range(IN_U):
                low_part(pool, v)
            pool.wait_ge(low_ok, IN_U)
            for g in range(G):
                inverse_deviation(pool, chain, G + g)
            for v in range(IN_U, BEFORE_SCATTER):
                low_part(pool, v)
            pool.wait_ge(low_ok, BEFORE_SCATTER)
            pool.wait_ge(pos_ok, 1)
            for t in range(TT):
                for k in range(2):
                    pool.indirect_dma_start(
                        out=rows_d, out_offset=bass.IndirectOffsetOnAxis(ap=pos_i[:, k, t:t + 1], axis=0),
                        in_=xn[:, t, :], in_offset=None).then_inc(scat_st, 16)

            def add_result(n, s, r):
                pool.tensor_copy(token_r[:, r:r + 1], token[:, n]).then_inc(token_ok, 1)
                pool.wait_ge(ysb_ok, s + 1)
                wait(pool, sum_st, s * 16 + 16 * -TT)
                pool.wait_ge(token_ok, s + (1 - TT))
                pool.sem_inc(add_start, 1)
                pool.indirect_dma_start(
                    out=out_d, out_offset=bass.IndirectOffsetOnAxis(ap=token_r[:, r:r + 1], axis=0),
                    in_=ysb[:, r, :], in_offset=None, compute_op=ALU.add).then_inc(sum_st, 16)

            pool.wait_ge(slots_ok, 1)
            for r in range(2):
                pool.wait_ge(y_st[r], 16 * TT // 2)
            add_result(slice(0, 1), TT, 0)
            with pool.Fori(0, SLOT_TILES // 2) as j:
                for n in range(1, 3):
                    add_result(bass.ds(j * 2 + n, 1), j * 2 + (n + TT), n % 2)

        def transposed_to_sbuf(act, n):
            g = n % G
            act.wait_ge(xn_tr, n + 1)
            bank, end = (2, DB) if n < G else (4, 128)
            act.activation(xnT[:, 0, g * GT:(g + 1) * GT], ps[:, bank, :], ACT.Copy).then_inc(xnT_ok, 1)
            act.activation(xnT[0:end, 1, g * GT:(g + 1) * GT], ps[0:end, bank + 1, :], ACT.Copy).then_inc(xnT_ok, 1)
            if n >= G:
                act.wait_ge(xnT_ok, 2 * (n + 1))

        @block.scalar
        def _(act):
            link = [0]

            def chain(ins):
                link[0] += 1
                ins.then_inc(act_c, 1)
                act.wait_ge(act_c, link[0])

            act.dma_start(projT[:, :, :], projT_d.rearrange("(k p) d -> p k d", p=128)).then_inc(ld_proj, 16)
            act.dma_start(projb[:, :], projb_d.partition_broadcast(128)).then_inc(ld_pos, 16)
            for half in range(2):
                act.dma_start(posb[half * S:(half + 1) * S, :], pos_d).then_inc(ld_pos, 16)
            act.dma_start(inTa[:, :], inT_d[0:DA, :]).then_inc(ld_par, 16)
            act.dma_start(inTb[:, :], inT_d[DA:D, :]).then_inc(ld_par, 16)
            act.dma_start(par[:, :, :], par_d.rearrange("(i p) n -> p i n", p=128)).then_inc(ld_par, 16)
            act.dma_start(xpT[:, :, :], xpT_d.rearrange("(i p) n -> p i n", p=128)).then_inc(ld_mid, 16)
            act.dma_start(dtT[:, :], dtT_d).then_inc(ld_mid, 16)
            act.dma_start(outT[:, :, :], outT_d.rearrange("(i p) n -> p i n", p=128)).then_inc(ld_mid, 16)
            act.dma_start(gateTa[:, :], gateT_d[0:DA, :]).then_inc(ld_mid, 16)
            act.dma_start(gateTb[:, :], gateT_d[DA:D, :]).then_inc(ld_mid, 16)
            act.wait_ge(zero_ok, 1)
            for z in range(0, SLOT_TILES, 4):
                end = min(z + 4, SLOT_TILES)
                act.dma_start(rows_v[z:end].rearrange("s p d -> p s d"), zeros[:, 0:end - z, :]).then_inc(zero_st, 16)
            act.dma_start(sum_v[TT], zeros[:, 0, 0:D]).then_inc(spare_st, 16)
            def conv_silu(g, i):
                act.wait_ge(conv_ok, IC * g + i + 1)
                act.activation(h[:, g, i, :], u[:, g, i, :], ACT.Silu).then_inc(h_ok, 1)

            def projected(n):
                g, m = ORDER[n]
                act.wait_ge(in_mm, n + 1)
                if m < IC:
                    act.activation(hp[:, g, m, :, K - 1:],
                                   ps[:, PROJ_BANK[n], :].rearrange("p (b s) -> p b s", b=GB),
                                   ACT.Copy).then_inc(hidden_ok, 1)
                else:
                    act.activation(sg[:, g, m - IC, :], ps[:, PROJ_BANK[n], :], ACT.Silu).then_inc(hidden_ok, 1)

            def dt_linear(g):
                for i in range(IC):
                    act.wait_ge(dt_mm, IC * g + i + 1)
                    act.activation(dt[:, g, i, :], ps[:, 1 + i, :], ACT.Identity, bias=par[:, i, P_DTB:P_DTB + 1])
                    act.activation(u[:, g, i, :], ps[:, 1 + i, :], ACT.Abs,
                                   bias=par[:, i, P_DTB:P_DTB + 1]).then_inc(dt_lin, 1)
                act.wait_ge(dt_lin, IC * (g + 1))

            def dt_exp(g):
                chain(act.activation(u[:, g, :, :], u[:, g, :, :], ACT.Exp, scale=-1.0))

            def dt_ln(g):
                for i in range(IC):
                    act.activation(u[:, g, i, :], u[:, g, i, :], ACT.Ln, bias=1.0).then_inc(lnp_ok, 1)

            act.wait_ge(ld_par, 48)
            act.activation(negA[:, :, :], par[:, :, P_A:P_A + N], ACT.Exp).then_inc(expA_ok, 1)
            act.wait_ge(pads_ok, 1)
            transposed_to_sbuf(act, 0)
            for n in range(0, IC):
                projected(n)
            transposed_to_sbuf(act, 1)
            for i in range(IC):
                conv_silu(0, i)
                projected(IC + i)
            act.wait_ge(h_ok, IC)
            dt_linear(0)
            dt_exp(0)
            dt_ln(0)

            def decays_of(g, n, jj):
                r, i = n // IC, n % IC
                act.wait_ge(decay_free, STEPS * g + n + 1 + jj * (2 * IC))
                scales = negA[:, i, :].rearrange("p (j r q) -> p j r q", r=2, q=NQ)
                for q in range(NQ):
                    last = act.activation(
                        decay(n % 2)[:, q, :, 1:],
                        dt[:, g, i, :].rearrange("p (b s) -> p b s", b=GB)[:, :, 1:], ACT.Exp,
                        scale=scales[:, jj, r, q:q + 1])
                last.then_inc(decay_ok, 1)

            act.wait_ge(negA_ok, 1)
            for s in range(STEPS):
                act.wait_ge(dt_ok, min(s + 1, IC))
                decays_of(0, s % (2 * IC), s // (2 * IC))
                if s == 1:
                    for i in range(IC):
                        conv_silu(1, i)
                    for n in range(2 * IC, 4 * IC - GATES_LATE):
                        projected(n)
                    act.wait_ge(h_ok, IC * G)
                if s == 6:
                    dt_linear(1)
                if s == 6:
                    dt_exp(1)
                if s == 7:
                    dt_ln(1)
                if s == 9:
                    for n in range(4 * IC - GATES_LATE, 4 * IC):
                        projected(n)
            act.wait_ge(dt_ok, IC * G)
            with act.Fori(0, Q // 2) as jj:
                for n in range(2 * IC):
                    decays_of(1, n, jj)
            act.wait_ge(u_ok, IC * G)
            act.wait_ge(decay_ok, G * STEPS)
            act.wait_ge(state_free, STEPS + 3 + 1)
            for v in range(IN_H_DT):
                high_part(act, v)
            act.wait_ge(state_free, G * STEPS + 3)
            for v in range(IN_H_DT, IN_U):
                high_part(act, v)
            transposed_to_sbuf(act, G)

            def x_high(s, r):
                wait(act, up_c, s - 1)
                if isinstance(s, int) and s < TT:
                    source = xnT[:, :, 128 * s:128 * (s + 1)]
                else:
                    act.wait_ge(xs_tr, s + (1 - TT))
                    source = ps[:, 4, 0:256].rearrange("p (k n) -> p k n", k=2)
                act.activation(xs_high[:, r, :, :], source, ACT.Copy).then_inc(x_high_ok, 1)

            def silu(s, r):
                act.wait_ge(up_a, s + 1)
                wait(act, hm_ok, s - 1)
                act.activation(sa[:, r, :], ps[:, r, :], ACT.Silu).then_inc(sa_ok, 1)

            def h_copy(s, r):
                act.wait_ge(hm_tr, s + 1)
                act.activation(hT[:, r, :, :], ps[:, 5, :].rearrange("p (c n) -> p c n", c=HC),
                               ACT.Copy).then_inc(hT_ok, 1)

            def between(s):
                if s == -1:
                    for v in range(IN_U, BEFORE_SCATTER):
                        high_part(act, v)
                    transposed_to_sbuf(act, G + 1)
                if s == 0:
                    act.wait_ge(lmax_ok, 1)
                    act.activation(sc[:, :, :], lg[:, :, :], ACT.Exp).then_inc(lexp_ok, 1)
                for v in late_halves(s):
                    high_part(act, v)

            stage_loop(act, [(1, silu), (2, x_high), (0, h_copy)], between)

        @block.vector
        def _(dve):
            link = [0]

            def chain(ins):
                link[0] += 1
                ins.then_inc(dve_c, 1)
                dve.wait_ge(dve_c, link[0])

            def summed_rows(g, add, added, last_norm=None):
                tiles = range(TPG * g, TPG * (g + 1))
                for t in tiles:
                    add(t)
                    if t > tiles[0]:
                        dve.wait_ge(added, t)
                        dve.bn_stats(stats[:, t - 1, :], h0[:, t - 1, :])
                    if last_norm and t == tiles[last_norm[1]]:
                        normed(last_norm[0])
                dve.wait_ge(added, TPG * (g + 1))
                chain(dve.bn_stats(stats[:, t, :], h0[:, t, :]))
                for t in tiles:
                    last = dve.bn_aggr(mv[:, t, :], stats[:, t, :])
                last.then_inc(aggr_ok, 1)

            def normed(n):
                dve.wait_ge(rstd_ok, n + 1)
                for t in range(TPG * (n % G), TPG * (n % G) + TPG):
                    dve.tensor_scalar(xn[:, t, 0:D], h0[:, t, :], mv[:, t, 0:1], rstd[:, t:t + 1],
                                      ALU.subtract, ALU.mult).then_inc(xn_ok, 1)
                if n >= G:
                    dve.wait_ge(xn_ok, TPG * (n + 1))
                    tiles = slice(TPG * (n % G), TPG * (n % G) + TPG)
                    dve.tensor_copy(xn[:, tiles, D:2 * DA], xn[:, tiles, DA:D]).then_inc(ends_ok, 1)

            dve.memset(hp[:, :, :, :, 0:K - 1].rearrange("p g i b s -> p (g i b) s"), 0.0).then_inc(pads_ok, 1)
            dve.wait_ge(ld_pos, 48)
            chain(dve.tensor_tensor(posb[:, :], posb[:, :], projb[:, :], ALU.add))
            def embedded(t):
                dve.wait_ge(patch_mm, t + 1)
                dve.tensor_tensor(h0[:, t, :], ps[:, t % 2, 0:D], posb[:, :], ALU.add).then_inc(h0_ok, 1)

            summed_rows(0, embedded, h0_ok)
            summed_rows(1, embedded, h0_ok, (0, 0))
            normed(1)
            dve.wait_ge(consts_ok, 3)
            chain(dve.tensor_copy(iota[:, :], iota_i[:, :]))
            dve.tensor_scalar(steps[:, :], iota[:, 0:TT], 128.0, None, ALU.mult)
            dve.memset(msum[:, :, 0:1], 0.0)
            dve.tensor_scalar(same_expert[:, :, :], iota[:, 0:TT + 1].unsqueeze(1).to_broadcast([128, E, TT + 1]),
                              0.0, None, ALU.is_gt)
            dve.wait_ge(ld_par, 48)
            def scan_coefficients(g):
                dve.wait_ge(xp_mm, g + 1)
                dve.tensor_copy(ssm[:, g, :], ps[0:R + 2 * N, 0, :]).then_inc(ssm_ok, 1)

            def convolved(g, i):
                dve.wait_ge(hidden_ok, IC * g + i + 1)
                out = u[:, g, i, :].rearrange("p (b s) -> p b s", b=GB)
                chain(dve.tensor_scalar(out, hp[:, g, i, :, 0:S], par[:, i, P_CW:P_CW + 1],
                                        par[:, i, P_CB:P_CB + 1], ALU.mult, ALU.add))
                for k in range(1, K):
                    ins = dve.scalar_tensor_tensor(out, hp[:, g, i, :, k:k + S], par[:, i, P_CW + k:P_CW + k + 1],
                                                   out, ALU.mult, ALU.add)
                    if k == K - 1:
                        ins.then_inc(conv_ok, 1)
                    else:
                        chain(ins)

            for i in range(IC):
                convolved(0, i)
            convolved(1, 0)
            scan_coefficients(0)
            for i in range(1, IC):
                convolved(1, i)
            dve.wait_ge(ident_ok, 2)
            dve.wait_ge(conv_ok, IC * G)
            for r in range(2):
                dve.memset(decay(r)[:, :, :, 0:1].rearrange("p n b s -> p (n b) s"), 0.0).then_inc(decay_free, 1)
            for i in range(IC):
                dve.tensor_scalar(diagD[:, i, :], ident[:, :], par[:, i, P_D:P_D + 1], None,
                                  ALU.mult).then_inc(diag_ok, 1)
            dve.wait_ge(expA_ok, 1)
            dve.tensor_scalar(negA[:, :, :], negA[:, :, :], -1.0, None, ALU.mult).then_inc(negA_ok, 1)

            def time_steps(g):
                for i in range(IC):
                    dve.wait_ge(lnp_ok, IC * g + i + 1)
                    chain(dve.scalar_tensor_tensor(dt[:, g, i, :], dt[:, g, i, :], 0.0, u[:, g, i, :],
                                                   ALU.max, ALU.add))
                    end = dt[:, g, i, S - 1::S]
                    dve.tensor_scalar(end, end, par[:, i, P_ALPHA:P_ALPHA + 1], None, ALU.mult).then_inc(dt_ok, 1)
                    if g == 0:
                        dve.wait_ge(dt_ok, i + 1)
                        dve.tensor_tensor(u[:, 0, i, :], dt[:, 0, i, :], h[:, 0, i, :], ALU.mult).then_inc(u_ok, 1)

            def scanned(g, n, jj):
                r, s = n // IC, STEPS * g + n
                dve.wait_ge(decay_ok, s + 1 + jj * (2 * IC))
                dve.wait_ge(dbu_ok, s + 1 + jj * (2 * IC))
                dve.tensor_tensor_scan(state(n % 3), decays[:, n % 2, :], state(n % 3), 0.0,
                                       ALU.mult, ALU.add).then_inc(decay_free, 1)
                dve.wait_ge(decay_free, s + 3 + jj * (2 * IC))
                if n % IC == 0:
                    dve.wait_ge(c_ld[r], 16 * (Q // 2) * g + 16 + jj * 16)
                dve.tensor_tensor(state(n % 3), state(n % 3),
                                  bc[:, r, 1, :, :].rearrange("p n t -> p (n t)"), ALU.mult).then_inc(cs_ok, 1)

            time_steps(0)
            for s in range(STEPS):
                scanned(0, s % (2 * IC), s // (2 * IC))
                if s == 3:
                    scan_coefficients(1)
                if s == 9:
                    time_steps(1)
            with dve.Fori(0, Q // 2) as jj:
                for n in range(2 * IC):
                    scanned(1, n, jj)
            dve.wait_ge(hidden_ok, 2 * IC * G)
            for g in range(G):
                dve.wait_ge(state_free, STEPS * (g + 1) + 3)
                for i in range(IC):
                    dve.tensor_tensor(sg[:, g, i, :], ps[:, YBANK[g] + i, :], sg[:, g, i, :],
                                      ALU.mult).then_inc(yevac, 1)
                dve.wait_ge(yevac, IC * (g + 1))
                for i in range(IC):
                    end = sg[:, g, i, S - 1::S]
                    dve.tensor_scalar(end, end, par[:, i, P_FG:P_FG + 1], None, ALU.mult).then_inc(y_ok, 1)
            dve.wait_ge(xn_tr, G)
            def with_output(t):
                dve.wait_ge(op_mm, t + 1)
                dve.tensor_tensor(h0[:, t, :], ps[:, OBANK[t % 2], 0:D], h0[:, t, :], ALU.add).then_inc(h1_ok, 1)

            summed_rows(0, with_output, h1_ok)
            summed_rows(1, with_output, h1_ok, (G, 1))

            def over_e(ap):
                return ap.unsqueeze(2).to_broadcast([128, TT, E])

            def second_rows():
                normed(G + 1)

            def shifted_logits():
                dve.wait_ge(lg_mm, G)
                chain(dve.tensor_copy(lg[:, :, :], ps[:, 7, 0:TT * E].rearrange("p (t e) -> p t e", t=TT)))
                chain(dve.tensor_reduce(red[:, 0, :], lg[:, :, :], AX.X, ALU.max))
                dve.tensor_tensor(lg[:, :, :], lg[:, :, :], over_e(red[:, 0, :]), ALU.subtract).then_inc(lmax_ok, 1)

            def top_two():
                dve.wait_ge(lexp_ok, 1)
                chain(dve.tensor_reduce(red[:, 1, :], sc[:, :, :], AX.X, ALU.add))
                chain(dve.reciprocal(red[:, 1, :], red[:, 1, :]))
                chain(dve.tensor_tensor(sc[:, :, :], sc[:, :, :], over_e(red[:, 1, :]), ALU.mult))
                for t in range(TT):
                    last = dve.max(m8[:, t, :], sc[:, t, :])
                chain(last)
                for t in range(TT):
                    last = dve.max_index(ix[:, t, :], m8[:, t, :], sc[:, t, :])
                chain(last)

            def one_hots():
                chain(dve.tensor_copy(ixf[:, :, :], ix[:, :, 0:2].rearrange("p t k -> p k t")))
                chain(dve.tensor_tensor(
                    hot[:, :, :, :].rearrange("p k t e -> p (k t) e"),
                    iota[:, 0:E].unsqueeze(1).to_broadcast([128, 2 * TT, E]),
                    ixf[:, :, :].rearrange("p k t -> p (k t)").unsqueeze(2).to_broadcast([128, 2 * TT, E]),
                    ALU.is_equal))
                chain(dve.tensor_tensor(msum[:, :, 1:].rearrange("p e t -> p t e"), hot[:, 0, :, :], hot[:, 1, :, :],
                                        ALU.add))
                dve.tensor_tensor_scan(mcum[:, :, :].rearrange("p e t -> p (e t)"),
                                       same_expert[:, :, :].rearrange("p e t -> p (e t)"),
                                       msum[:, :, :].rearrange("p e t -> p (e t)"), 0.0,
                                       ALU.mult, ALU.add).then_inc(mcum_ok, 1)

            def token_weights():
                chain(dve.tensor_tensor(red[:, 2, :], m8[:, :, 0], m8[:, :, 1], ALU.add))
                chain(dve.tensor_scalar(red[:, 2, :], red[:, 2, :], 1e-20, None, ALU.add))
                chain(dve.reciprocal(red[:, 2, :], red[:, 2, :]))
                dve.wait_ge(ids_ok, 1)
                dve.tensor_copy(xn[:, :, FIRST_EXPERT], ixf[:, 0, :])
                for k in range(2):
                    last = dve.tensor_tensor(xn[:, :, WEIGHT + k], m8[:, :, k], red[:, 2, :], ALU.mult)
                chain(last)

            def tile_counts():
                dve.wait_ge(rank_mm, 1)
                ranks = ps[:, 4, 0:E * (TT + 1)].rearrange("p (e t) -> p e t", e=E)
                dve.tensor_copy(rank[:, :, :], ranks[:, :, 0:TT].rearrange("p e t -> p t e"))
                chain(dve.tensor_copy(cnt[:, :], ranks[:, :, TT]))
                gt_v = gt[:, :].rearrange("p (e k) -> p e k", k=TT)
                chain(dve.tensor_tensor(gt_v, cnt[:, :].unsqueeze(2).to_broadcast([128, E, TT]),
                                        steps[:, :].unsqueeze(1).to_broadcast([128, E, TT]), ALU.is_gt))
                chain(dve.tensor_reduce(ntile[:, :], gt_v, AX.X, ALU.add))
                chain(dve.tensor_tensor_scan(tend[:, :], ones[:, 0:E], ntile[:, :], 0.0, ALU.mult, ALU.add))
                chain(dve.tensor_tensor(base[:, :], tend[:, :], ntile[:, :], ALU.subtract))

            def slots():
                chain(dve.tensor_scalar(base[:, :], base[:, :], 128.0, None, ALU.mult))
                chain(dve.tensor_tensor(rank[:, :, :], rank[:, :, :],
                                        base[:, :].unsqueeze(1).to_broadcast([128, TT, E]), ALU.add))
                for k in range(2):
                    last = dve.tensor_tensor(hot[:, k, :, :], hot[:, k, :, :], rank[:, :, :], ALU.mult)
                chain(last)
                chain(dve.tensor_reduce(posf[:, :, :], hot[:, :, :, :], AX.X, ALU.add))
                dve.tensor_copy(pos_i[:, :, :], posf[:, :, :]).then_inc(pos_ok, 1)

            def tile_experts():
                chain(dve.tensor_tensor(tcmp[:, :, :], iota[:, :].unsqueeze(2).to_broadcast([128, SLOT_TILES, E]),
                                        tend[:, :].unsqueeze(1).to_broadcast([128, SLOT_TILES, E]), ALU.is_ge))
                chain(dve.tensor_reduce(tef[:, :], tcmp[:, :, :], AX.X, ALU.add))
                chain(dve.tensor_scalar(tef[:, :], tef[:, :], float(E - 1), None, ALU.min))
                dve.tensor_copy(te[:, :], tef[:, :]).then_inc(te_ok, 1)

            def slot_weights():
                dve.wait_ge(info_ld, 16)
                dve.tensor_copy(token[:, :], info[:, :, TOKEN - 2 * DA])
                for k, same in enumerate((ALU.is_equal, ALU.not_equal)):
                    last = dve.tensor_tensor(chosen[:, k, :], info[:, :, FIRST_EXPERT - 2 * DA], tef[:, :], same)
                chain(last)
                for k in range(2):
                    last = dve.tensor_tensor(chosen[:, k, :], chosen[:, k, :], info[:, :, WEIGHT + k - 2 * DA],
                                             ALU.mult)
                chain(last)
                dve.tensor_tensor(weight[:, :], chosen[:, 0, :], chosen[:, 1, :], ALU.add).then_inc(slots_ok, 1)
                dve.wait_ge(slots_ok, 1)
                for r in range(2):
                    dve.wait_ge(y_st[r], 16 * TT // 2)

            def x_low(s, r):
                dve.wait_ge(x_high_ok, s + 1)
                if isinstance(s, int) and s < TT:
                    source = xnT[:, :, 128 * s:128 * (s + 1)]
                else:
                    source = ps[:, 4, 0:256].rearrange("p (k n) -> p k n", k=2)
                dve.tensor_tensor(xs_low[:, r, :, :], source, xs_high[:, r, :, :].bitcast(F32),
                                  ALU.subtract).then_inc(x_low_ok, 1)

            def gated(s, r):
                dve.wait_ge(up_c, s + 1)
                dve.wait_ge(sa_ok, s + 1)
                dve.tensor_tensor(hm[:, r, :], ps[:, 2 + r, :], sa[:, r, :], ALU.mult).then_inc(hm_ok, 1)

            def result(s, r):
                dve.wait_ge(down_mm, s + 1)
                if isinstance(s, int) and s < TT:
                    wait(dve, y_st[r], 16 * (s // 2))
                    dve.tensor_tensor(ysb[:, r, :], ps[:, 6 + r, 0:D], h0[:, s, :], ALU.add).then_inc(ysb_ok, 1)
                    return
                if not isinstance(s, int) or s >= TT + 2:
                    dve.wait_ge(sum_st, s * 16 + -16 * (TT + 1))
                n = slice(s - TT, s - TT + 1) if isinstance(s, int) else bass.ds(s + -TT, 1)
                dve.tensor_tensor(ysb[:, r, :], ps[:, 6 + r, 0:D], weight[:, n].to_broadcast([128, D]),
                                  ALU.mult).then_inc(ysb_ok, 1)

            def between(s):
                for stage in {-1: (second_rows,), 0: (shifted_logits, top_two), 1: (one_hots, token_weights),
                              2: (tile_counts, slots), 3: (tile_experts,), TT + 1: (slot_weights,)}.get(s, ()):
                    stage()
                for v in late_halves(s):
                    low_part(dve, v)

            stage_loop(dve, [(1, gated), (2, x_low), (-1, result)], between)

        @block.tensor
        def _(pe):
            def transposes(n):
                g = n % G
                if n:
                    pe.wait_ge(xnT_ok, 2 * n)
                bank, end = (2, DB) if n < G else (4, 128)
                for q in range(TPG):
                    pe.wait_ge(xn_ok, TPG * n + q + 1)
                    pe.transpose(ps[:, bank, 128 * q:128 * (q + 1)], xn[:, TPG * g + q, 0:DA], ident[:, :])
                if n >= G:
                    pe.wait_ge(ends_ok, n - G + 1)
                for q in range(TPG):
                    last = pe.transpose(ps[0:end, bank + 1, 128 * q:128 * (q + 1)], xn[:, TPG * g + q, DA:DA + end],
                                        ident[:, :])
                last.then_inc(xn_tr, 1)

            pe.wait_ge(ld_proj, 16)
            for t in range(TT):
                if t <= TPG:
                    pe.wait_ge(ld_x[t], 16)
                if t >= 2:
                    pe.wait_ge(h0_ok, t - 1)
                for k in range(PK):
                    last = pe.matmul(ps[:, t % 2, 0:D], xT[:, k, 128 * t:128 * (t + 1)], projT[:, k, :],
                                     start=(k == 0), stop=(k == PK - 1))
                last.then_inc(patch_mm, 1)
                if t == TPG + 2:
                    pe.wait_ge(ident_ok, 2)
                    transposes(0)

            PROJ_FREE = {4: (hidden_ok, 1), 5: (hidden_ok, 2), 6: (hidden_ok, 4), 7: (ssm_ok, 1), 8: (dt_lin, IC),
                         11: (hidden_ok, 7)}

            def project(n):
                g, m = ORDER[n]
                if n in PROJ_FREE:
                    pe.wait_ge(*PROJ_FREE[n])
                pe.matmul(ps[:, PROJ_BANK[n], :], inTa[:, 128 * m:128 * (m + 1)], xnT[:, 0, GT * g:GT * (g + 1)],
                          start=True, stop=False)
                pe.matmul(ps[:, PROJ_BANK[n], :], inTb[:, 128 * m:128 * (m + 1)], xnT[0:DB, 1, GT * g:GT * (g + 1)],
                          start=False, stop=True).then_inc(in_mm, 1)

            def coefficients(g):
                if g:
                    pe.wait_ge(hidden_ok, 4 * IC - GATES_LATE)
                for i in range(IC):
                    pe.wait_ge(h_ok, IC * g + i + 1)
                    last = pe.matmul(ps[0:R + 2 * N, 0, :], xpT[:, i, :], h[:, g, i, :],
                                     start=(i == 0), stop=(i == IC - 1))
                last.then_inc(xp_mm, 1)

            def time_step_products(g):
                pe.wait_ge(ssm_ok, g + 1)
                if g:
                    pe.wait_ge(dt_lin, IC * g)
                for i in range(IC):
                    pe.matmul(ps[:, 1 + i, :], dtT[:, 128 * i:128 * (i + 1)], ssm[0:R, g, :],
                              start=True, stop=True).then_inc(dt_mm, 1)

            pe.wait_ge(xnT_ok, 2)
            pe.wait_ge(ld_par, 48)
            for n in range(IC):
                project(n)
            transposes(1)
            pe.wait_ge(xnT_ok, 2 * G)
            for n in range(IC, 2 * IC):
                project(n)
            pe.wait_ge(ld_mid, 80)
            pe.wait_ge(h0_ok, TT)
            coefficients(0)
            time_step_products(0)
            for n in range(2 * IC, 4 * IC - GATES_LATE):
                project(n)
            pe.wait_ge(diag_ok, IC)

            def skip_terms(g):
                for i in range(IC):
                    pe.matmul(ps[:, YBANK[g] + i, :], diagD[:, i, :], h[:, g, i, :], start=True, stop=True)

            def summed(g, n, jj):
                pe.wait_ge(cs_ok, STEPS * g + n + 1 + jj * (2 * IC))
                for q in range(NQ):
                    last = pe.matmul(ps[:, YBANK[g] + n % IC, :], ident[:, :], state(n % 3)[:, q * GT:(q + 1) * GT],
                                     start=False, stop=True, skip_group_check=True)
                last.then_inc(state_free, 1)

            pe.wait_ge(hidden_ok, 2 * IC)
            skip_terms(0)
            for s in range(STEPS):
                summed(0, s % (2 * IC), s // (2 * IC))
                if s == 1:
                    coefficients(1)
                if s == 3:
                    time_step_products(1)
                if 4 <= s < 4 + GATES_LATE:
                    project(4 * IC - GATES_LATE + s - 4)
            pe.wait_ge(dt_lin, IC * G)
            pe.wait_ge(hidden_ok, 4 * IC)
            skip_terms(1)
            with pe.Fori(0, Q // 2) as jj:
                for n in range(2 * IC):
                    summed(1, n, jj)
            for t in range(TT):
                g, q = t // TPG, t % TPG
                if q == 0:
                    pe.wait_ge(y_ok, IC * (g + 1))
                if t >= 2:
                    pe.wait_ge(h1_ok, t - 1)
                for i in range(IC):
                    last = pe.matmul(ps[:, OBANK[t % 2], 0:D], sg[:, g, i, 128 * q:128 * (q + 1)], outT[:, i, :],
                                     start=(i == 0), stop=(i == IC - 1))
                last.then_inc(op_mm, 1)
            pe.wait_ge(h1_ok, TT)

            def logits(g):
                pe.wait_ge(xnT_ok, 2 * (G + g + 1))
                for t in range(TPG * g, TPG * (g + 1)):
                    o = ps[:, 7, t * E:(t + 1) * E]
                    pe.matmul(o, xnT[:, 0, 128 * t:128 * (t + 1)], gateTa[:, :], start=True, stop=False)
                    last = pe.matmul(o, xnT[0:DB, 1, 128 * t:128 * (t + 1)], gateTb[:, :], start=False, stop=True)
                last.then_inc(lg_mm, 1)

            def x_transposes(s, r):
                if isinstance(s, int) and s < TT:
                    return
                pe.wait_ge(xs_ld[r], s * 8 + (16 - 8 * r - 8 * TT))
                pe.wait_ge(x_low_ok, s)
                pe.transpose(ps[:, 4, 0:128], xs[:, r, 0:DA], ident[:, :])
                pe.transpose(ps[:, 4, 128:256], xs[:, r, DA:], ident[:, :]).then_inc(xs_tr, 1)

            def expert(weights, s):
                if isinstance(s, int) and s < TT:
                    return weights[:, 0]
                n = slice(s - TT, s - TT + 1) if isinstance(s, int) else bass.ds(s + -TT, 1)
                return weights[:, 1:E + 1][:, pe.value_load(te[0:1, n], min_val=0, max_val=E - 1)]

            def up(s, r):
                we = expert(w13, s)
                pe.wait_ge(x_low_ok, s + 1)
                wait(pe, hm_ok, s - 1)
                high, low = xs_high[:, r, :, :], xs_low[:, r, :, :]
                for c, done in ((0, up_a), (1, up_c)):
                    o = ps[:, 2 * c + r, :]
                    wh, wl, ends = (we[:, k, c * HID:(c + 1) * HID] for k in range(3))
                    pe.matmul(o, high[:, 0, :], wh, start=True, stop=False)
                    pe.matmul(o, high[:, 0, :], wl, start=False, stop=False)
                    pe.matmul(o, low[:, 0, :], wh, start=False, stop=False)
                    pe.matmul(o, low[:, 0, :], wl, start=False, stop=False)
                    pe.matmul(o, high[:, 1, :], ends, start=False, stop=False)
                    pe.matmul(o, low[:, 1, :], ends, start=False, stop=True).then_inc(done, 1)

            def h_transposes(s, r):
                pe.wait_ge(hm_ok, s + 1)
                wait(pe, hT_ok, s)
                for c in range(HC):
                    last = pe.transpose(ps[:, 5, 128 * c:128 * (c + 1)], hm[:, r, 128 * c:128 * (c + 1)], ident[:, :])
                last.then_inc(hm_tr, 1)

            def down(s, r):
                we = expert(w2, s)
                pe.wait_ge(hT_ok, s + 1)
                wait(pe, ysb_ok, s - 1)
                for c in range(HC):
                    last = pe.matmul(ps[:, 6 + r, 0:D], hT[:, r, c, :], we[:, c * D:(c + 1) * D],
                                     start=(c == 0), stop=(c == HC - 1))
                last.then_inc(down_mm, 1)

            def between(s):
                if s == -2:
                    transposes(G)
                    logits(0)
                    transposes(G + 1)
                    pe.wait_ge(ld_w2, 16 * (E + 1))
                    pe.wait_ge(low_ok, 2)
                if s == 0:
                    logits(1)
                if s == 2:
                    pe.wait_ge(mcum_ok, 1)
                    pe.wait_ge(consts_ok, 3)
                    o = ps[:, 4, 0:E * (TT + 1)]
                    pe.matmul(o, ones[:, :], mcum[:, :, :].rearrange("p e t -> p (e t)"), start=True, stop=True)
                    pe.matmul(o.rearrange("p (e t) -> p e t", e=E)[:, :, 0:TT], before[:, :], msum[:, :, 1:],
                              start=False, stop=True, skip_group_check=True).then_inc(rank_mm, 1)
                if s == TT - 1:
                    pe.wait_ge(te_ok, 1)
                    pe.wait_ge(low_ok, len(HALVES))

            stage_loop(pe, [(1, up), (2, x_transposes), (0, h_transposes), (-1, down)], between)


_ARRAYS = ("xT", "projT", "projb", "pos", "inT", "params", "xpT", "dtT", "outT", "gateT", "w13T", "w2T")


def kernel(x, L0_tok_proj_w, L0_tok_proj_b, L0_tok_pos_emb, L0_attn_in_proj_w, L0_attn_conv_w, L0_attn_conv_b,
           L0_attn_x_proj_w, L0_attn_dt_proj_w, L0_attn_dt_proj_b, L0_attn_A_log, L0_attn_D, L0_attn_out_proj_w,
           L0_attn_alpha, L0_attn_feature_gating, L0_ffn_gate_w, L0_ffn_w1, L0_ffn_w2, L0_ffn_w3,
           L0_ffn_ws1, L0_ffn_ws2, L0_ffn_ws3):
    import concourse.bacc as bacc
    from concourse.bass_utils import run_bass_kernel_spmd

    a = np.asarray
    col = lambda v: a(v).reshape(I, 1)
    side = IMG // PATCH
    w1 = np.concatenate([a(L0_ffn_ws1)[None], a(L0_ffn_w1)]).transpose(0, 2, 1)
    w3 = np.concatenate([a(L0_ffn_ws3)[None], a(L0_ffn_w3)]).transpose(0, 2, 1)
    laid = {
        "xT": (a(x).reshape(B, C_IN, side, PATCH, side, PATCH).transpose(0, 1, 2, 4, 3, 5)
               .reshape(T, PD).T),
        "projT": a(L0_tok_proj_w).T,
        "projb": a(L0_tok_proj_b),
        "pos": a(L0_tok_pos_emb)[0],
        "inT": a(L0_attn_in_proj_w).T,
        "params": np.concatenate([a(L0_attn_conv_w)[:, 0], col(L0_attn_conv_b), col(L0_attn_dt_proj_b),
                                  a(L0_attn_A_log), col(L0_attn_D), col(L0_attn_alpha),
                                  col(L0_attn_feature_gating)], axis=1),
        "xpT": a(L0_attn_x_proj_w).T,
        "dtT": a(L0_attn_dt_proj_w).T,
        "outT": a(L0_attn_out_proj_w).T,
        "gateT": a(L0_ffn_gate_w).T,
        "w13T": np.concatenate([w1, w3], axis=2),
        "w2T": np.concatenate([a(L0_ffn_ws2)[None], a(L0_ffn_w2)]).transpose(0, 2, 1),
    }
    laid = {n: np.ascontiguousarray(v) for n, v in laid.items()}
    nc = bacc.Bacc("TRN2", target_bir_lowering=False, num_devices=1)
    args = [nc.dram_tensor("in_" + n, laid[n].shape, F32, kind="ExternalInput").ap() for n in _ARRAYS]
    out = nc.dram_tensor("out", (T + 128, D), F32, kind="ExternalOutput").ap()
    program(nc, *args, out)
    r = run_bass_kernel_spmd(nc, [{"in_" + n: v for n, v in laid.items()}], core_ids=[0])
    return r.results[0]["out"][0:T].reshape(B, S, D)
```
